# Optimizing a Trainium2 kernel written in Bass

```python
import numpy as np
import jax
import jax.numpy as jnp

def _softmax(x, axis=-1):
    return jax.nn.softmax(x, axis=axis)

def _gelu(x):
    return jax.nn.gelu(x, approximate=True)

def _silu(x):
    return jax.nn.silu(x)

def _sigmoid(x):
    return jax.nn.sigmoid(x)

def _layernorm(x, axis=-1, eps=1e-05):
    m = jnp.mean(x, axis=axis, keepdims=True)
    v = jnp.var(x, axis=axis, keepdims=True)
    return (x - m) / jnp.sqrt(v + eps)

def _scatter_add(tgt, idx, src, axis=0):
    return tgt.at[idx].add(src)

def _segment_sum(src, seg, n):
    return jax.ops.segment_sum(src, seg, n)
kernel_name = 'mk_vit_tower_d2_tok_img512_r4_131fbf'

def setup_inputs(seed: int=0):
    np.random.seed(seed)
    _w = jnp.asarray

    def _rec_inputs():
        import jax
        import jax.numpy as jnp
        _rk = jax.random.key(seed)
        x = -0.000477451 + 1.00034 * jax.random.normal(jax.random.fold_in(_rk, 1), (16, 32, 32, 29), jnp.float32)
        return x
    x = _rec_inputs()

    def _L0_tok_setup():
        import jax, jax.numpy as jnp
        import numpy as np
        import math
        H, W_DIM, D_MODEL, B = (32, 32, 128, 128)
        F_TOTAL = 29
        SEQ_LEN = H * W_DIM

        def make_pe(seq_len: int, d_model: int) -> jnp.ndarray:
            position = np.arange(seq_len, dtype=np.float32)[:, None]
            div_term = np.exp(np.arange(0, d_model, 2, dtype=np.float32) * (-math.log(10000.0) / d_model))
            pe = np.zeros((seq_len, d_model), dtype=np.float32)
            pe[:, 0::2] = np.sin(position * div_term)
            pe[:, 1::2] = np.cos(position * div_term)
            return jnp.asarray(pe)
        key = jax.random.key(seed)
        k1, k2 = jax.random.split(key)
        state_tensor = jax.random.normal(k1, (B, H, W_DIM, F_TOTAL), dtype=jnp.float32)
        W = jax.random.normal(k2, (F_TOTAL, D_MODEL), dtype=jnp.float32) * 0.05
        return {'state_tensor': state_tensor, 'W': W}
    _L0_tok_all = _L0_tok_setup()
    _L0_tok_in = {k: v for k, v in _L0_tok_all.items() if k in ('W',)}
    del _L0_tok_all

    def _L0_attn_setup():
        import jax, jax.numpy as jnp
        import numpy as np
        B, S, C = (2, 1024, 128)
        H, D = (8, 64)
        G = 32
        EPS = 1e-06

        def group_norm(x, w, b):
            b_, s_, c_ = x.shape
            xg = x.reshape(b_, s_, G, c_ // G)
            mean = jnp.mean(xg, axis=(1, 3), keepdims=True)
            var = jnp.var(xg, axis=(1, 3), keepdims=True)
            xn = (xg - mean) * jax.lax.rsqrt(var + EPS)
            xn = xn.reshape(b_, s_, c_)
            return xn * w + b
        key = jax.random.key(seed)
        ks = jax.random.split(key, 10)
        inner = H * D
        sc = 0.02
        return {'hidden_states': jax.random.normal(ks[0], (B, S, C), dtype=jnp.float32), 'gn_w': jnp.ones((C,), dtype=jnp.float32), 'gn_b': jnp.zeros((C,), dtype=jnp.float32), 'wq': jax.random.normal(ks[1], (C, inner), dtype=jnp.float32) * sc, 'bq': jnp.zeros((inner,), dtype=jnp.float32), 'wk': jax.random.normal(ks[2], (C, inner), dtype=jnp.float32) * sc, 'bk': jnp.zeros((inner,), dtype=jnp.float32), 'wv': jax.random.normal(ks[3], (C, inner), dtype=jnp.float32) * sc, 'bv': jnp.zeros((inner,), dtype=jnp.float32), 'wo': jax.random.normal(ks[4], (inner, C), dtype=jnp.float32) * sc, 'bo': jnp.zeros((C,), dtype=jnp.float32)}
    _L0_attn_all = _L0_attn_setup()
    _L0_attn_in = {k: v for k, v in _L0_attn_all.items() if k in ('gn_w', 'gn_b', 'wq', 'bq', 'wk', 'bk', 'wv', 'bv', 'wo', 'bo')}
    del _L0_attn_all

    def _L0_ffn_setup():
        import jax, jax.numpy as jnp
        import numpy as np
        T = 128
        B = 64
        C = 256

        def _triu_apply(x, W, b):
            Wm = jnp.tril(W)
            return jnp.einsum('bct,st->bcs', x, Wm) + b
        key = jax.random.key(seed)
        ks = jax.random.split(key, 5)
        x = jax.random.normal(ks[0], (B, C, T), dtype=jnp.float32)
        scale = 1.0 / jnp.sqrt(jnp.arange(1, T + 1, dtype=jnp.float32))[:, None]
        W1 = jax.random.uniform(ks[1], (T, T), jnp.float32, -1.0, 1.0) * scale
        b1 = jax.random.uniform(ks[2], (T,), jnp.float32, -1.0, 1.0) * scale[:, 0]
        W2 = jax.random.uniform(ks[3], (T, T), jnp.float32, -1.0, 1.0) * scale
        b2 = jax.random.uniform(ks[4], (T,), jnp.float32, -1.0, 1.0) * scale[:, 0]
        return {'x': x, 'W1': W1, 'b1': b1, 'W2': W2, 'b2': b2}
    _L0_ffn_all = _L0_ffn_setup()
    _L0_ffn_in = {k: v for k, v in _L0_ffn_all.items() if k in ('W1', 'b1', 'W2', 'b2')}
    del _L0_ffn_all

    def _L1_attn_setup():
        import jax, jax.numpy as jnp
        import numpy as np
        import math
        D_MODEL = 128
        NUM_HEADS = 8
        D_HEAD = D_MODEL // NUM_HEADS
        key = jax.random.key(seed)
        ks = jax.random.split(key, 8)
        B, S = (2, 512)
        x = jax.random.normal(ks[0], (B, S, D_MODEL), dtype=jnp.float32)
        s = 1.0 / math.sqrt(D_MODEL)
        Wq = jax.random.normal(ks[1], (NUM_HEADS, D_MODEL, D_HEAD), dtype=jnp.float32) * s
        Wk = jax.random.normal(ks[2], (NUM_HEADS, D_MODEL, D_HEAD), dtype=jnp.float32) * s
        Wv = jax.random.normal(ks[3], (NUM_HEADS, D_MODEL, D_HEAD), dtype=jnp.float32) * s
        bq = jax.random.normal(ks[4], (NUM_HEADS, D_HEAD), dtype=jnp.float32) * 0.02
        bk = jax.random.normal(ks[5], (NUM_HEADS, D_HEAD), dtype=jnp.float32) * 0.02
        bv = jax.random.normal(ks[6], (NUM_HEADS, D_HEAD), dtype=jnp.float32) * 0.02
        Wo = jax.random.normal(ks[7], (D_MODEL, D_MODEL), dtype=jnp.float32) * s
        bo = jnp.zeros((D_MODEL,), dtype=jnp.float32)
        return {'x': x, 'Wq': Wq, 'Wk': Wk, 'Wv': Wv, 'bq': bq, 'bk': bk, 'bv': bv, 'Wo': Wo, 'bo': bo}
    _L1_attn_all = _L1_attn_setup()
    _L1_attn_in = {k: v for k, v in _L1_attn_all.items() if k in ('Wq', 'Wk', 'Wv', 'bq', 'bk', 'bv', 'Wo', 'bo')}
    del _L1_attn_all

    def _L1_ffn_setup():
        import jax, jax.numpy as jnp
        import numpy as np
        CAPACITY_FACTOR = 1.2
        key = jax.random.key(seed)
        k1, k2, k3 = jax.random.split(key, 3)
        B, S, D, E = (8, 1024, 128, 16)
        x = jax.random.normal(k1, (B, S, D), dtype=jnp.float32)
        switch_w = jax.random.normal(k2, (E, D), dtype=jnp.float32) * 0.02
        switch_b = jnp.zeros((E,), dtype=jnp.float32)
        expert_w = jax.random.normal(k3, (E, D, D), dtype=jnp.float32) * 0.02
        expert_b = jnp.zeros((E, D), dtype=jnp.float32)
        return {'x': x, 'switch_w': switch_w, 'switch_b': switch_b, 'expert_w': expert_w, 'expert_b': expert_b}
    _L1_ffn_all = _L1_ffn_setup()
    _L1_ffn_in = {k: v for k, v in _L1_ffn_all.items() if k in ('switch_w', 'switch_b', 'expert_w', 'expert_b')}
    del _L1_ffn_all
    return {'x': x, 'L0_tok_W': _L0_tok_in['W'], 'L0_attn_gn_w': _L0_attn_in['gn_w'], 'L0_attn_gn_b': _L0_attn_in['gn_b'], 'L0_attn_wq': _L0_attn_in['wq'], 'L0_attn_bq': _L0_attn_in['bq'], 'L0_attn_wk': _L0_attn_in['wk'], 'L0_attn_bk': _L0_attn_in['bk'], 'L0_attn_wv': _L0_attn_in['wv'], 'L0_attn_bv': _L0_attn_in['bv'], 'L0_attn_wo': _L0_attn_in['wo'], 'L0_attn_bo': _L0_attn_in['bo'], 'L0_ffn_W1': _L0_ffn_in['W1'], 'L0_ffn_b1': _L0_ffn_in['b1'], 'L0_ffn_W2': _L0_ffn_in['W2'], 'L0_ffn_b2': _L0_ffn_in['b2'], 'L1_attn_Wq': _L1_attn_in['Wq'], 'L1_attn_Wk': _L1_attn_in['Wk'], 'L1_attn_Wv': _L1_attn_in['Wv'], 'L1_attn_bq': _L1_attn_in['bq'], 'L1_attn_bk': _L1_attn_in['bk'], 'L1_attn_bv': _L1_attn_in['bv'], 'L1_attn_Wo': _L1_attn_in['Wo'], 'L1_attn_bo': _L1_attn_in['bo'], 'L1_ffn_switch_w': _L1_ffn_in['switch_w'], 'L1_ffn_switch_b': _L1_ffn_in['switch_b'], 'L1_ffn_expert_w': _L1_ffn_in['expert_w'], 'L1_ffn_expert_b': _L1_ffn_in['expert_b']}

def reference(x, L0_tok_W, L0_attn_gn_w, L0_attn_gn_b, L0_attn_wq, L0_attn_bq, L0_attn_wk, L0_attn_bk, L0_attn_wv, L0_attn_bv, L0_attn_wo, L0_attn_bo, L0_ffn_W1, L0_ffn_b1, L0_ffn_W2, L0_ffn_b2, L1_attn_Wq, L1_attn_Wk, L1_attn_Wv, L1_attn_bq, L1_attn_bk, L1_attn_bv, L1_attn_Wo, L1_attn_bo, L1_ffn_switch_w, L1_ffn_switch_b, L1_ffn_expert_w, L1_ffn_expert_b):
    import jax
    import jax.numpy as jnp

    def _L0_tok_ref(state_tensor, W):
        import jax, jax.numpy as jnp
        import numpy as np
        import math
        H, W_DIM, D_MODEL, B = (32, 32, 128, 128)
        F_TOTAL = 29
        SEQ_LEN = H * W_DIM

        def make_pe(seq_len: int, d_model: int) -> jnp.ndarray:
            position = np.arange(seq_len, dtype=np.float32)[:, None]
            div_term = np.exp(np.arange(0, d_model, 2, dtype=np.float32) * (-math.log(10000.0) / d_model))
            pe = np.zeros((seq_len, d_model), dtype=np.float32)
            pe[:, 0::2] = np.sin(position * div_term)
            pe[:, 1::2] = np.cos(position * div_term)
            return jnp.asarray(pe)
        b, h, w, f = state_tensor.shape
        s = h * w
        x = state_tensor.reshape(b, s, f)
        emb = jnp.einsum('bsf,fd->bsd', x, W)
        pe = make_pe(s * 2, W.shape[1])[:s]
        return emb + pe[None, :, :]

    def _L0_attn_ref(hidden_states, gn_w, gn_b, wq, bq, wk, bk, wv, bv, wo, bo):
        import jax, jax.numpy as jnp
        import numpy as np
        B, S, C = (2, 1024, 128)
        H, D = (8, 64)
        G = 32
        EPS = 1e-06

        def group_norm(x, w, b):
            b_, s_, c_ = x.shape
            xg = x.reshape(b_, s_, G, c_ // G)
            mean = jnp.mean(xg, axis=(1, 3), keepdims=True)
            var = jnp.var(xg, axis=(1, 3), keepdims=True)
            xn = (xg - mean) * jax.lax.rsqrt(var + EPS)
            xn = xn.reshape(b_, s_, c_)
            return xn * w + b
        residual = hidden_states
        b_, s_, _ = hidden_states.shape
        x = group_norm(hidden_states, gn_w, gn_b)
        q = (x @ wq + bq).reshape(b_, s_, H, D)
        k = (x @ wk + bk).reshape(b_, s_, H, D)
        v = (x @ wv + bv).reshape(b_, s_, H, D)
        scale = D ** (-0.5)
        scores = jnp.einsum('bqhd,bkhd->bhqk', q, k) * scale
        attn = jax.nn.softmax(scores, axis=-1)
        out = jnp.einsum('bhqk,bkhd->bqhd', attn, v).reshape(b_, s_, H * D)
        return out @ wo + bo + residual

    def _L0_ffn_ref(x, W1, b1, W2, b2):
        import jax, jax.numpy as jnp
        import numpy as np
        T = 128
        B = 64
        C = 256

        def _triu_apply(x, W, b):
            Wm = jnp.tril(W)
            return jnp.einsum('bct,st->bcs', x, Wm) + b
        h = _triu_apply(x, W1, b1)
        h = jax.nn.gelu(h, approximate=False)
        return _triu_apply(h, W2, b2)

    def _L1_attn_ref(x, Wq, Wk, Wv, bq, bk, bv, Wo, bo):
        import jax, jax.numpy as jnp
        import numpy as np
        import math
        D_MODEL = 128
        NUM_HEADS = 8
        D_HEAD = D_MODEL // NUM_HEADS
        Q = jnp.einsum('bsd,hde->bhse', x, Wq) + bq[None, :, None, :]
        K = jnp.einsum('bsd,hde->bhse', x, Wk) + bk[None, :, None, :]
        V = jnp.einsum('bsd,hde->bhse', x, Wv) + bv[None, :, None, :]
        scale = 1.0 / math.sqrt(D_HEAD)
        scores = jnp.einsum('bhqe,bhke->bhqk', Q, K) * scale
        attn = jax.nn.softmax(scores, axis=-1)
        out = jnp.einsum('bhqk,bhke->bhqe', attn, V)
        B, H, S, d = out.shape
        concat = out.transpose(0, 2, 1, 3).reshape(B, S, H * d)
        return jnp.einsum('bsd,de->bse', concat, Wo) + bo

    def _L1_ffn_ref(x, switch_w, switch_b, expert_w, expert_b):
        import jax, jax.numpy as jnp
        import numpy as np
        CAPACITY_FACTOR = 1.2
        B, S, D = x.shape
        E = switch_w.shape[0]
        N = B * S
        xf = x.reshape(N, D)
        logits = xf @ switch_w.T + switch_b
        probs = jax.nn.softmax(logits, axis=-1)
        route_probs = jnp.max(probs, axis=-1)
        routes = jnp.argmax(probs, axis=-1)
        oh = jax.nn.one_hot(routes, E, dtype=jnp.int32)
        pos = jnp.take_along_axis(jnp.cumsum(oh, axis=0), routes[:, None], axis=1)[:, 0] - 1
        capacity = int(CAPACITY_FACTOR * N / E)
        keep = pos < capacity
        buf = jnp.zeros((E, capacity, D), dtype=xf.dtype).at[routes, pos].set(xf)
        y = jnp.einsum('ecd,efd->ecf', buf, expert_w) + expert_b[:, None, :]
        gathered = y[routes, jnp.minimum(pos, capacity - 1)]
        out = jnp.where(keep[:, None], gathered, xf) * route_probs[:, None]
        return out.reshape(B, S, D)
    h = _L0_tok_ref(x, L0_tok_W)
    h = h + _L0_attn_ref(_layernorm(h, axis=-1), L0_attn_gn_w, L0_attn_gn_b, L0_attn_wq, L0_attn_bq, L0_attn_wk, L0_attn_bk, L0_attn_wv, L0_attn_bv, L0_attn_wo, L0_attn_bo)
    h = h + _L0_ffn_ref(_layernorm(h, axis=-1), L0_ffn_W1, L0_ffn_b1, L0_ffn_W2, L0_ffn_b2)
    h = h + _L1_attn_ref(_layernorm(h, axis=-1), L1_attn_Wq, L1_attn_Wk, L1_attn_Wv, L1_attn_bq, L1_attn_bk, L1_attn_bv, L1_attn_Wo, L1_attn_bo)
    h = h + _L1_ffn_ref(_layernorm(h, axis=-1), L1_ffn_switch_w, L1_ffn_switch_b, L1_ffn_expert_w, L1_ffn_expert_b)
    return h

_drawn_inputs = setup_inputs


def setup_inputs(seed=0):
    import zlib

    import numpy as np

    out = dict(_drawn_inputs(seed))
    spreads = {'L0_attn_gn_w': (1.0, 0.6),
     'L0_attn_gn_b': (0.0, 0.8),
     'L0_attn_bq': (0.0, 0.8),
     'L0_attn_bk': (0.0, 2.0),
     'L0_attn_bv': (0.0, 0.1),
     'L0_attn_bo': (0.0, 0.1),
     'L1_attn_bo': (0.0, 0.1),
     'L1_ffn_switch_b': (0.0, 0.311),
     'L1_ffn_expert_b': (0.0, 0.8)}
    factors = {'L0_attn_wq': 8.0,
     'L0_attn_wk': 8.0,
     'L1_attn_bq': 37.147,
     'L1_attn_bk': 64.0,
     'L1_attn_bv': 4.183,
     'L1_ffn_expert_w': 5.37}
    for name, (base, spread) in spreads.items():
        noise = np.random.default_rng([zlib.crc32(name.encode()), seed]).standard_normal(out[name].shape)
        drawn = base * np.exp(spread * noise) if base else spread * noise
        out[name] = jnp.asarray(drawn.astype(out[name].dtype))
    for name, factor in factors.items():
        out[name] = (out[name] * factor).astype(out[name].dtype)
    return out
```

```python
from contextlib import ExitStack
import math

import numpy as np

import concourse.bass as bass
from concourse import mybir

F32 = mybir.dt.float32
F32R = mybir.dt.float32r
BF16 = mybir.dt.bfloat16
ALU = mybir.AluOpType
ACT = mybir.ActivationFunctionType
AX_X = mybir.AxisListType.X

P = 128


class Counts:

    def __init__(self, sem, per_turn, credit=0):
        self.sem, self.per_turn, self.credit, self.made = sem, per_turn, credit, 0

    def at(self, turn, count):
        return turn * self.per_turn + (count + self.credit)


def glue_plan():
    uses = ["xT0", "xT1", "h0", "h1", "zT0.0", "zT0.1", "gn_mean", "gn_var"]
    uses += [f"v0.{t}" for t in range(8)]
    uses += [f"{w}{c}.{g}" for c in (0,) for w in "qk" for g in range(2)]
    uses += ["m0.0"]
    for h in range(8):
        if h % 2 == 0 and h < 6:
            uses += [f"{w}{h // 2 + 1}.{g}" for w in "qk" for g in range(2)]
        if h < 7:
            uses += [f"m0.{h + 1}"]
    for g in range(2):
        uses += [f"oT{t}" for t in range(4 * g, 4 * g + 4)] + [f"attn0.{g}"]
    uses += ["zT1.0", "zT1.1", "ffn_h0", "ffn_h1", "ffn_o0", "ffn_o1", "zT2.0", "zT2.1"]
    uses += ["q1.0", "q1.1", "k1.0", "k1.1", "v1.0", "v1.1", "m1.0"]
    uses += [f"m1.{h}" for h in range(1, 8)]
    uses += ["oT1.0", "oT1.1", "attn1.0", "attn1.1", "zT3.0", "zT3.1", "logits", "rank", "wT0", "wT1", "eb0", "eb1"]
    for t in range(0, 8, 2):
        for q in range(4):
            uses += [f"e{t}.{q}", f"e{t + 1}.{q}"]
    names = {}
    fixed = []
    for u in uses:
        n = names.get(u, 0)
        names[u] = n + 1
        fixed.append(u if n == 0 else u + "'" * n)
    if len(fixed) % 2:
        fixed.append("pad")
    return {u: (n % 2, n // 2) for n, u in enumerate(fixed)}, len(fixed) // 2


def build(nc, x, tok_w, gn_w, gn_b, wq, bq, wk, bk, wv, bv, wo, bo, w1, b1, w2, b2,
          wq1, wk1, wv1, bq1, bk1, bv1, wo1, bo1, sw, sb_, ew, eb, pe, tri, out):
    NB, HH, WW, FT = x.shape
    S = HH * WW
    T = S // P
    C = tok_w.shape[1]
    H0, D0 = 8, 64
    H1, D1 = wq1.shape[0], wq1.shape[2]
    E = sw.shape[0]
    CAP = float(int(1.2 * (NB * S) / E))
    INNER = H0 * D0
    NCH = INNER // P
    HALF = S // 2
    assert C == P and T == 8 and D0 == 64 and H1 * D1 == P and E * T == P

    with ExitStack() as ctx:
        def sb(name, shape, dt=F32):
            return ctx.enter_context(nc.sbuf_tensor(name, shape, dt))

        def sem(name):
            return ctx.enter_context(nc.semaphore(name))

        tri_sb = sb("tri_sb", [P, 5, P])
        ident, group4, before, lower, desc = (tri_sb[:, n, :] for n in range(5))
        ones = sb("ones", [P, P])
        pool_c = sb("pool_c", [P, 3, T])
        pe_sb = sb("pe_sb", [P, T, C])
        tokw_sb = sb("tokw_sb", [FT, C])
        wq_sb = sb("wq_sb", [P, INNER])
        wk_sb = sb("wk_sb", [P, INNER])
        wv_sb = sb("wv_sb", [P, INNER])
        wo_sb = sb("wo_sb", [P, NCH, C])
        w1T = sb("w1T", [P, P])
        w2T = sb("w2T", [P, P])
        wq1_sb = sb("wq1_sb", [P, P])
        wk1_sb = sb("wk1_sb", [P, P])
        wv1_sb = sb("wv1_sb", [P, P])
        wo1_sb = sb("wo1_sb", [P, P])
        swT = sb("swT", [P, E])
        ewT = sb("ewT", [P, E, P])
        eb_sb = sb("eb_sb", [E, P])
        cols = sb("cols", [P, 24])
        gnw_c, gnb_c, b1_c, bq1_c, bk1_c = (cols[:, n:n + 1] for n in range(5))
        bq_c, bk_c, bv_c, bv1_c = cols[:, 5:9], cols[:, 9:13], cols[:, 13:17], cols[:, 17:18]
        rows = sb("rows", [1, 4 * P])
        bo_b = sb("bo_b", [P, C])
        b2_b = sb("b2_b", [P, C])
        bo1_b = sb("bo1_b", [P, C])
        sb_b = sb("sb_b", [P, E])

        xin = sb("xin", [P, T, FT])
        h = sb("h", [P, T, C])
        z = sb("z", [P, T, C])
        zT = sb("zT", [P, S])
        xT = sb("xT", [P, S])
        st = sb("st", [P, T, 6])
        mv = sb("mv", [P, T, 2])
        rs = sb("rs", [P, T])
        gst = sb("gst", [P, 2, 6])
        gmv = sb("gmv", [P, 2])
        gsm = sb("gsm", [P, 8])
        v0 = sb("v0", [P, T, H0, 2 * D0 + 2], BF16)
        v1 = sb("v1", [P, T, H1, 2 * D1 + 2], BF16)
        q_hi = sb("q_hi", [P, 2, S], F32R)
        q_lo = sb("q_lo", [P, 2, S], F32R)
        k_hi = sb("k_hi", [P, 2, S], F32R)
        k_lo = sb("k_lo", [P, 2, S], F32R)
        kA = sb("kA", [P, 2, S], F32R)
        qA = sb("qA", [P, 2, S], F32R)
        kB = sb("kB", [65, 2, S], F32R)
        qB = sb("qB", [65, 2, S], F32R)
        pr = sb("pr", [P, 2, T, HALF])
        pr_lo = sb("pr_lo", [P, 2, T, HALF], BF16)
        mxh = sb("mxh", [P, 2, T, 2])
        mx = sb("mx", [P, 2, T])
        mrow = sb("mrow", [T, 2, P], F32R)
        o_hi = sb("o_hi", [P, 2, 2, D0])
        o_r = sb("o_r", [P, 4, 2])
        on = sb("on", [P, T, INNER])
        oT = sb("oT", [P, 2, INNER])
        lg = sb("lg", [P, T, E])
        ex = sb("ex", [P, T, E])
        oh = sb("oh", [P, T, E])
        prefix = sb("prefix", [P, T, E])
        wgt = sb("wgt", [P, T, E])
        small = sb("small", [P, 8, T])
        seen = sb("seen", [P, E])
        per_p = sb("per_p", [P, E])

        banks = [ctx.enter_context(nc.psum_tensor(f"bank{n}", [P, 512], F32)) for n in range(8)]
        glue, score, maxb, obank = banks[0:2], banks[2:4], banks[4:6], banks[6:8]

        plan, glue_uses = glue_plan()
        load_small = sem("load_small")
        prep_pe = sem("prep_pe")
        prep_dve = sem("prep_dve")
        prep_pool = sem("prep_pool")
        x_loaded = Counts(sem("x_loaded"), 16)
        out_stored = Counts(sem("out_stored"), 16)
        h_free = Counts(sem("h_free"), 1, credit=1)
        glue_filled = [Counts(sem(f"glue_filled{b}"), glue_uses) for b in range(2)]
        glue_drained = [Counts(sem(f"glue_drained{b}"), glue_uses, credit=1) for b in range(2)]
        z_ready = Counts(sem("z_ready"), 8)
        stats_ready = Counts(sem("stats_ready"), 4)
        rstd_ready = Counts(sem("rstd_ready"), 5)
        gn_stat = Counts(sem("gn_stat"), 2)
        xn_ready = Counts(sem("xn_ready"), 1)
        parts_hi = Counts(sem("parts_hi"), 8 + 16 + 4 + 2)
        stacks_in = [Counts(sem(f"stacks_in{n}"), 16 * 4 * (6 + 8)) for n in range(2)]
        max_filled = Counts(sem("max_filled"), 256)
        max_reduced = Counts(sem("max_reduced"), 256, credit=2)
        max_ready = Counts(sem("max_ready"), 16)
        mrow_in = [Counts(sem(f"mrow_in{n}"), 16 * 8) for n in range(2)]
        score_filled = Counts(sem("score_filled"), 256)
        exp_done = Counts(sem("exp_done"), 256, credit=2)
        lo_done = Counts(sem("lo_done"), 128)
        o_filled = Counts(sem("o_filled"), 64)
        o_hi_out = Counts(sem("o_hi_out"), 64)
        o_drained = Counts(sem("o_drained"), 64, credit=2)
        on_ready = Counts(sem("on_ready"), 64)
        res_ready = Counts(sem("res_ready"), 3)
        logit_ready = Counts(sem("logit_ready"), 1)
        ex_ready = Counts(sem("ex_ready"), 1)
        oh_ready = Counts(sem("oh_ready"), 1)
        prefix_ready = Counts(sem("prefix_ready"), 7)
        wgt_ready = Counts(sem("wgt_ready"), 1)
        dve_link = Counts(sem("dve_link"), DVE_LINKS)
        pool_link = Counts(sem("pool_link"), POOL_LINKS)

        x_v = x.rearrange("b h w f -> b (h w) f").rearrange("b (p t) f -> b p t f", t=T)
        out_v = out.rearrange("b (p t) c -> b p t c", t=T)

        def await_drained(eng, i, *names):
            for name in names:
                b, k = plan[name]
                eng.wait_ge(glue_drained[b].sem, glue_drained[b].at(i, k + 1))

        QK0 = {(w, c, g): f"{w}{c}.{g}" for w in "qk" for c in range(NCH) for g in range(2)}
        QK1 = {(w, g): f"{w}1.{g}'" for w in "qk" for g in range(2)}

        def oT4(t):
            return oT[:, t % 4, :] if t % 4 < 2 else xT[:, (t % 4 - 2) * 512:(t % 4 - 1) * 512]

        block = ctx.enter_context(nc.Block())

        @block.sync
        def _(sp):
            small_loads = [
                (tri_sb[:, :, :], tri), (tokw_sb[:, :], tok_w), (wq_sb[:, :], wq), (wk_sb[:, :], wk), (wv_sb[:, :], wv),
                (pe_sb[:, :, :], pe), (wo_sb[:, :, :], wo.rearrange("(c p) n -> p c n", p=P)),
                (pr[:, 0, 0, 0:P], w1), (pr[:, 0, 0, P:2 * P], w2), (wo1_sb[:, :], wo1), (eb_sb[:, :], eb),
                (wq1_sb[:, :].rearrange("p (h e) -> p h e", e=D1), wq1.rearrange("h d e -> d h e")),
                (wk1_sb[:, :].rearrange("p (h e) -> p h e", e=D1), wk1.rearrange("h d e -> d h e")),
                (wv1_sb[:, :].rearrange("p (h e) -> p h e", e=D1), wv1.rearrange("h d e -> d h e")),
                (pr[0:E, 0, 1, 0:P], sw),
                (pr[:, 0, 2:6, :].rearrange("p a (e d) -> p (a e) d", d=P), ew.rearrange("e f d -> f e d")),
                (cols[:, 0:1], gn_w.rearrange("(p n) -> p n", n=1)), (cols[:, 1:2], gn_b.rearrange("(p n) -> p n", n=1)),
                (cols[:, 2:3], b1.rearrange("(p n) -> p n", n=1)),
                (cols[:, 3:4], bq1.rearrange("h e -> (h e)").rearrange("(p n) -> p n", n=1)),
                (cols[:, 4:5], bk1.rearrange("h e -> (h e)").rearrange("(p n) -> p n", n=1)),
                (cols[:, 5:9], bq.rearrange("(c p) -> p c", p=P)), (cols[:, 9:13], bk.rearrange("(c p) -> p c", p=P)),
                (cols[:, 13:17], bv.rearrange("(c p) -> p c", p=P)),
                (cols[:, 17:18], bv1.rearrange("h e -> (h e)").rearrange("(p n) -> p n", n=1)),
                (rows[:, 0:P], bo.rearrange("(a n) -> a n", a=1)), (rows[:, P:2 * P], b2.rearrange("(a n) -> a n", a=1)),
                (rows[:, 2 * P:3 * P], bo1.rearrange("(a n) -> a n", a=1)),
                (rows[:, 3 * P:3 * P + E], sb_.rearrange("(a n) -> a n", a=1)),
            ]
            assert len(small_loads) == N_SMALL
            with nc.allow_non_contiguous_dma(reason="a few biases as columns, once"):
                for dst, src in small_loads:
                    sp.dma_start(dst, src).then_inc(load_small, 16)
            slot_free = sp.alloc_register("slot_free")
            sp.wait_ge(prep_dve, PREP_DVE)
            with sp.Fori(0, NB) as i:
                sp.dma_start(xin[:, :, :], x_v[i]).then_inc(x_loaded.sem, 16)

                def stack(layer, head):
                    s = head % 2
                    n = 8 * layer + head
                    if n >= 2:
                        sp.reg_mov(slot_free, score_filled.at(i, 16 * (n - 1)))
                    if layer == 0 or head == 0:
                        await_drained(sp, i, QK0["k", head // 2, 1] if layer == 0 else QK1["k", 1])
                    if n >= 2:
                        sp.wait_ge(score_filled.sem, slot_free)
                    if layer == 0:
                        a, b_ = D0 * s, D0 * s + D0
                        moves = [(kA[0:D0, s], k_hi[a:b_, 0]), (kA[D0:P, s], k_lo[a:b_, 0]),
                                 (qA[0:D0, s], q_hi[a:b_, 0]), (qA[D0:P, s], q_hi[a:b_, 0]),
                                 (kB[0:D0, s], k_hi[a:b_, 0]), (qB[0:D0, s], q_lo[a:b_, 0])]
                    else:
                        a, b_ = D1 * head, D1 * head + D1
                        moves = []
                        for j in range(4):
                            r = slice(D1 * j, D1 * j + D1)
                            moves += [(kB[r, s], (k_hi, k_lo)[j % 2][a:b_, 1]), (qB[r, s], (q_hi, q_lo)[j // 2][a:b_, 1])]
                    for dst, src in moves:
                        sp.dma_start(dst.bitcast(F32), src.bitcast(F32)).then_inc(stacks_in[s].sem, 16)

                def row(layer, head):
                    await_drained(sp, i, f"m{layer}.{head}")
                    sp.dma_start(qB[64:65, head % 2, :].rearrange("a (t q) -> a t q", t=T).bitcast(F32),
                                 mrow[:, head % 2, :].bitcast(F32)).then_inc(mrow_in[head % 2].sem, 16)

                for layer in range(2):
                    stack(layer, 0)
                    row(layer, 0)
                    for head in range(1, 8):
                        stack(layer, head)
                        row(layer, head)

        def stack_count(layer, head):
            k = head // 2 + 1
            return 16 * (6 * k if layer == 0 else 24 + 8 * k)

        @block.tensor
        def _(te):
            mm = te.matmul
            te.wait_ge(load_small, 16 * N_SMALL)
            te.wait_ge(prep_dve, 4)
            for n in range(E):
                te.transpose(banks[n // 4][:, (n % 4) * P:(n % 4 + 1) * P],
                             pr[:, 0, 2 + n // 4, (n % 4) * P:(n % 4 + 1) * P], ident)
            te.transpose(banks[4][:, 0:P], pr[:, 1, 0, 0:P], ident)
            te.transpose(banks[4][:, P:2 * P], pr[:, 1, 0, P:2 * P], ident)
            te.transpose(banks[4][:, 2 * P:2 * P + E], pr[0:E, 0, 1, 0:P], ident[0:E, 0:E])
            for c in range(NCH):
                mm(banks[5][:, 0:P], pr[:, 1, 1, c * P:(c + 1) * P], wo_sb[:, c, :], start=(c == 0), stop=False)
            mm(banks[5][:, 0:P], ones[0:1, :], rows[:, 0:P], start=False, stop=True)
            mm(banks[6][:, 0:P], pr[:, 1, 2, 0:P], wo1_sb[:, :], start=True, stop=False)
            mm(banks[6][:, 0:P], ones[0:1, :], rows[:, 2 * P:3 * P], start=False, stop=True)
            mm(banks[7][:, 0:P], ones[0:1, :], rows[:, P:2 * P], start=True, stop=True)
            mm(banks[7][:, P:P + E], ones[0:1, :], rows[:, 3 * P:3 * P + E], start=True, stop=True).then_inc(prep_pe, 1)
            te.wait_ge(prep_dve, PREP_DVE)

            with te.Fori(0, NB) as i:
                def use(name):
                    b, k = plan[name]
                    te.wait_ge(glue_drained[b].sem, glue_drained[b].at(i, k))
                    return glue[b], glue_filled[b].sem

                def have_T(name):
                    await_drained(te, i, name)

                def turn(name, src, rows_=P):
                    bank, filled = use(name)
                    for j in range(4):
                        last = te.transpose(bank[0:rows_, j * P:(j + 1) * P], src(j), ident)
                    last.then_inc(filled, 1)

                def z_turns(n):
                    for g in range(2):
                        te.wait_ge(z_ready.sem, z_ready.at(i, 2 * n + g + 1))
                        turn(f"zT{n}.{g}", lambda j: z[:, 4 * g + j, :])

                te.wait_ge(x_loaded.sem, x_loaded.at(i, 16))
                for g in range(2):
                    turn(f"xT{g}", lambda j: xin[:, 4 * g + j, :], FT)
                for g in range(2):
                    have_T(f"xT{g}")
                    bank, filled = use(f"h{g}")
                    for j in range(4):
                        t = 4 * g + j
                        last = mm(bank[:, j * P:(j + 1) * P], xT[0:FT, t * P:(t + 1) * P], tokw_sb[:, :], start=True, stop=True)
                    last.then_inc(filled, 1)
                z_turns(0)
                for n, name in enumerate(("gn_mean", "gn_var")):
                    te.wait_ge(gn_stat.sem, gn_stat.at(i, n + 1))
                    bank, filled = use(name)
                    mm(bank[:, 0:1], group4, gsm[:, n:n + 1], start=True, stop=True).then_inc(filled, 1)
                te.wait_ge(xn_ready.sem, xn_ready.at(i, 1))
                for t in range(T):
                    bank, filled = use(f"v0.{t}")
                    mm(bank[:, :], zT[:, t * P:(t + 1) * P], wv_sb[:, :], start=True, stop=True).then_inc(filled, 1)

                def project(c):
                    for w, ws in (("q", wq_sb), ("k", wk_sb)):
                        for g in range(2):
                            bank, filled = use(QK0[w, c, g])
                            mm(bank[:, :], ws[:, c * P:(c + 1) * P], zT[:, g * HALF:(g + 1) * HALF],
                               start=True, stop=True).then_inc(filled, 1)

                def max_tile(layer, head, n):
                    k = 128 * layer + 16 * head + n
                    s, t, g = head % 2, n // 2, n % 2
                    if n == 0:
                        te.wait_ge(stacks_in[s].sem, stacks_in[s].at(i, stack_count(layer, head)))
                    te.wait_ge(max_reduced.sem, max_reduced.at(i, k - 1))
                    qs, ks = (qA[:, s], kA[:, s]) if layer == 0 else (qB[0:64, s], kB[0:64, s])
                    mm(maxb[k % 2][:, :], qs[:, t * P:(t + 1) * P], ks[:, g * HALF:(g + 1) * HALF],
                       start=True, stop=True).then_inc(max_filled.sem, 1)

                def max_turn(layer, head):
                    te.wait_ge(max_ready.sem, max_ready.at(i, 8 * layer + head + 1))
                    bank, filled = use(f"m{layer}.{head}")
                    te.transpose(bank[0:T, 0:P], mx[:, head % 2, :], ident).then_inc(filled, 1)

                def scores(layer, head, g, kt):
                    k = 128 * layer + 16 * head + 8 * g + kt
                    s = head % 2
                    if g == 0 and kt == 0:
                        te.wait_ge(mrow_in[s].sem, mrow_in[s].at(i, 16 * (4 * layer + head // 2 + 1)))
                    te.wait_ge(exp_done.sem, exp_done.at(i, k - 1))
                    bank, q, kk = score[k % 2], slice(g * HALF, (g + 1) * HALF), slice(kt * P, (kt + 1) * P)
                    if layer == 0:
                        mm(bank[:, :], kA[:, s, kk], qA[:, s, q], start=True, stop=False)
                    mm(bank[:, :], kB[:, s, kk], qB[:, s, q], start=(layer == 1), stop=True).then_inc(score_filled.sem, 1)

                def values(layer, u, j):
                    head = u // 2
                    n = 32 * layer + 2 * u + j // 2
                    v, w = (v0, 2 * D0 + 1) if layer == 0 else (v1, 2 * D1 + 1)
                    if j == 0:
                        te.wait_ge(lo_done.sem, lo_done.at(i, 64 * layer + 4 * u + 4))
                    if j % 2 == 0:
                        te.wait_ge(o_drained.sem, o_drained.at(i, n - 1))
                    dst = obank[n % 2][:, (j % 2) * 256:(j % 2) * 256 + w]
                    for kt in range(T):
                        hi = pr[:, u % 2, kt, j * P:(j + 1) * P].bitcast(BF16).rearrange("p (q two) -> p q two", two=2)[:, :, 1]
                        lo = pr_lo[:, u % 2, kt, j * P:(j + 1) * P]
                        mm(dst, hi, v[:, kt, head, 0:w], start=(kt == 0), stop=False)
                        last = mm(dst, lo, v[:, kt, head, 0:w], start=False, stop=(kt == T - 1))
                    if j % 2 == 1:
                        last.then_inc(o_filled.sem, 1)

                def attention(layer):
                    for n in range(16):
                        max_tile(layer, 0, n)
                    max_turn(layer, 0)
                    for head in range(8):
                        for g in range(2):
                            u = 2 * head + g
                            for kt in range(T):
                                step = 8 * g + kt
                                scores(layer, head, g, kt)
                                if head < 7:
                                    for n in MAX_STEPS[step]:
                                        max_tile(layer, head + 1, n)
                                if u >= 1 and kt % 2 == 1:
                                    if u == 1 and kt == 1:
                                        await_drained(te, i, *(("v0.6", "v0.7"), ("v1.0", "v1.1"))[layer])
                                    values(layer, u - 1, kt // 2)
                        if layer == 0 and head % 2 == 0 and head < 6:
                            project(head // 2 + 1)
                        if head < 7:
                            max_turn(layer, head + 1)
                    for j in range(4):
                        values(layer, 15, j)

                project(0)
                attention(0)
                for g in range(2):
                    te.wait_ge(on_ready.sem, on_ready.at(i, 32))
                    for j in range(4):
                        t = 4 * g + j
                        turn(f"oT{t}", lambda c: on[:, t, c * P:(c + 1) * P])
                    bank_name = f"attn0.{g}"
                    bank, filled = use(bank_name)
                    for j in range(4):
                        t = 4 * g + j
                        have_T(f"oT{t}")
                        for c in range(NCH):
                            last = mm(bank[:, j * P:(j + 1) * P], oT4(t)[:, c * P:(c + 1) * P], wo_sb[:, c, :],
                                      start=(c == 0), stop=(c == NCH - 1))
                    last.then_inc(filled, 1)
                z_turns(1)
                for g in range(2):
                    have_T(f"zT1.{g}")
                    bank, filled = use(f"ffn_h{g}")
                    mm(bank[:, :], w1T[:, :], zT[:, g * HALF:(g + 1) * HALF], start=True, stop=True).then_inc(filled, 1)
                for g in range(2):
                    have_T(f"ffn_h{g}")
                    bank, filled = use(f"ffn_o{g}")
                    for j in range(4):
                        t = 4 * g + j
                        last = mm(bank[:, j * P:(j + 1) * P], xT[:, t * P:(t + 1) * P], w2T[:, :], start=True, stop=True)
                    last.then_inc(filled, 1)
                z_turns(2)
                have_T("zT2.1")
                for w, ws in (("q", wq1_sb), ("k", wk1_sb)):
                    for g in range(2):
                        bank, filled = use(QK1[w, g])
                        mm(bank[:, :], ws[:, :], zT[:, g * HALF:(g + 1) * HALF], start=True, stop=True).then_inc(filled, 1)
                for g in range(2):
                    bank, filled = use(f"v1.{g}")
                    for j in range(4):
                        t = 4 * g + j
                        last = mm(bank[:, j * P:(j + 1) * P], zT[:, t * P:(t + 1) * P], wv1_sb[:, :], start=True, stop=True)
                    last.then_inc(filled, 1)
                attention(1)
                te.wait_ge(on_ready.sem, on_ready.at(i, 64))
                for g in range(2):
                    turn(f"oT1.{g}", lambda j: on[:, 4 * g + j, 0:P])
                for g in range(2):
                    have_T(f"oT1.{g}")
                    bank, filled = use(f"attn1.{g}")
                    for j in range(4):
                        last = mm(bank[:, j * P:(j + 1) * P], oT[:, g, j * P:(j + 1) * P], wo1_sb[:, :], start=True, stop=True)
                    last.then_inc(filled, 1)
                z_turns(3)
                have_T("zT3.1")
                bank, filled = use("logits")
                for t in range(T):
                    last = mm(bank[:, t * E:(t + 1) * E], zT[:, t * P:(t + 1) * P], swT[:, :], start=True, stop=True)
                last.then_inc(filled, 1)
                te.wait_ge(oh_ready.sem, oh_ready.at(i, 1))
                bank, filled = use("rank")
                mm(bank[:, 0:E], before, per_p[:, :], start=True, stop=True)
                mm(bank[:, E:2 * E], ones[:, :], per_p[:, :], start=True, stop=True).then_inc(filled, 1)
                te.wait_ge(wgt_ready.sem, wgt_ready.at(i, 1))
                for g in range(2):
                    turn(f"wT{g}", lambda j: wgt[:, 4 * g + j, :], E)
                for g in range(2):
                    have_T(f"wT{g}")
                    bank, filled = use(f"eb{g}")
                    for j in range(4):
                        t = 4 * g + j
                        last = mm(bank[:, j * P:(j + 1) * P], xT[0:E, t * P:(t + 1) * P], eb_sb[:, :], start=True, stop=True)
                    last.then_inc(filled, 1)
                for t0 in range(0, T, 2):
                    for q in range(4):
                        for t in (t0, t0 + 1):
                            bank, filled = use(f"e{t}.{q}")
                            mm(bank[:, :], zT[:, t * P:(t + 1) * P], ewT[:, 4 * q:4 * q + 4, :].rearrange("p e f -> p (e f)"),
                               start=True, stop=True).then_inc(filled, 1)
                if "pad" in plan:
                    bank, filled = use("pad")
                    mm(bank[:, 0:1], ident, ones[:, 0:1], start=True, stop=True).then_inc(filled, 1)

        @block.scalar
        def _(act):
            with act.Fori(0, NB) as i:
                def full(name):
                    b, k = plan[name]
                    act.wait_ge(glue_filled[b].sem, glue_filled[b].at(i, k + 1))
                    return glue[b], glue_drained[b].sem

                def move_T(name, dst, rows_=P):
                    bank, drained = full(name)
                    act.activation(dst, bank[0:rows_, :], ACT.Copy).then_inc(drained, 1)

                for g in range(2):
                    move_T(f"xT{g}", xT[0:FT, g * HALF:(g + 1) * HALF], FT)

                def z_copies(n):
                    for g in range(2):
                        move_T(f"zT{n}.{g}", zT[:, g * HALF:(g + 1) * HALF])

                z_copies(0)
                for t in range(T):
                    bank, _ = full(f"v0.{t}")
                    act.activation(v0[:, t, :, 0:D0], bank[:, :].rearrange("p (h d) -> p h d", d=D0), ACT.Copy)\
                        .then_inc(parts_hi.sem, 1)

                def project(c):
                    for w, dst, bias in (("q", q_hi, bq_c), ("k", k_hi, bk_c)):
                        for g in range(2):
                            bank, _ = full(QK0[w, c, g])
                            if g == 0 and w == "q" and c >= 1:
                                act.wait_ge(stacks_in[1].sem, stacks_in[1].at(i, stack_count(0, 2 * c - 1)))
                            act.activation(dst[:, 0, g * HALF:(g + 1) * HALF], bank[:, :], ACT.Identity, bias=bias[:, c:c + 1])\
                                .then_inc(parts_hi.sem, 1)

                def max_rows(layer, head):
                    bank, drained = full(f"m{layer}.{head}")
                    n = 8 * layer + head
                    if n >= 2:
                        act.wait_ge(mrow_in[head % 2].sem, mrow_in[head % 2].at(i, 16 * (n // 2)))
                    act.activation(mrow[:, head % 2, :], bank[0:T, 0:P], ACT.Copy, scale=-1.0).then_inc(drained, 1)

                def exps(layer, head, g, kt, scale):
                    k = 128 * layer + 16 * head + 8 * g + kt
                    u = 2 * head + g
                    act.wait_ge(score_filled.sem, score_filled.at(i, k + 1))
                    if kt == 0 and (layer, u) not in ((0, 0), (0, 1)):
                        act.wait_ge(o_filled.sem, o_filled.at(i, 32 * layer + 2 * u - 2))
                    act.activation(pr[:, u % 2, kt, :], score[k % 2][:, :], ACT.Exp, scale=scale).then_inc(exp_done.sem, 1)

                def outputs(layer, u, jj, D):
                    n = 32 * layer + 2 * u + jj
                    act.wait_ge(o_filled.sem, o_filled.at(i, n + 1))
                    act.wait_ge(o_drained.sem, o_drained.at(i, n - 1))
                    src = obank[n % 2][:, :].rearrange("p (j n) -> p j n", j=2)[:, :, 0:D]
                    act.activation(o_hi[:, n % 2, :, 0:D], src, ACT.Copy).then_inc(o_hi_out.sem, 1)

                def attention(layer):
                    D, scale = (D0, D0 ** -0.5) if layer == 0 else (D1, 1.0 / math.sqrt(D1))
                    max_rows(layer, 0)
                    for head in range(8):
                        for g in range(2):
                            u = 2 * head + g
                            for kt in range(T):
                                exps(layer, head, g, kt, scale)
                                if u >= 1 and kt % 4 == 3:
                                    outputs(layer, u - 1, kt // 4, D)
                        if layer == 0 and head % 2 == 0 and head < 6:
                            project(head // 2 + 1)
                        if head < 7:
                            max_rows(layer, head + 1)
                    for jj in range(2):
                        outputs(layer, 15, jj, D)

                project(0)
                attention(0)
                for g in range(2):
                    for j in range(4):
                        t = 4 * g + j
                        if g == 1 and j == 0:
                            b, k = plan["attn0.0"]
                            act.wait_ge(glue_filled[b].sem, glue_filled[b].at(i, k + 1))
                        move_T(f"oT{t}", oT4(t))
                z_copies(1)
                for g in range(2):
                    bank, drained = full(f"ffn_h{g}")
                    act.activation(xT[:, g * HALF:(g + 1) * HALF], bank[:, :], ACT.Gelu, bias=b1_c).then_inc(drained, 1)
                z_copies(2)
                for w, dst, bias in (("q", q_hi, bq1_c), ("k", k_hi, bk1_c)):
                    for g in range(2):
                        bank, _ = full(QK1[w, g])
                        act.activation(dst[:, 1, g * HALF:(g + 1) * HALF], bank[:, :], ACT.Identity, bias=bias)\
                            .then_inc(parts_hi.sem, 1)
                for g in range(2):
                    bank, _ = full(f"v1.{g}")
                    act.activation(v1[:, 4 * g:4 * g + 4, :, 0:D1], bank[:, :].rearrange("p (t h d) -> p t h d", t=4, d=D1),
                                   ACT.Copy).then_inc(parts_hi.sem, 1)
                attention(1)
                for g in range(2):
                    move_T(f"oT1.{g}", oT[:, g, :])
                z_copies(3)
                act.wait_ge(logit_ready.sem, logit_ready.at(i, 1))
                act.activation(ex[:, :, :], ex[:, :, :], ACT.Exp).then_inc(ex_ready.sem, 1)
                for g in range(2):
                    move_T(f"wT{g}", xT[0:E, g * HALF:(g + 1) * HALF], E)

        @block.gpsimd
        def _(pool):
            for n, value in enumerate((-0.5, 1e-5, 1e-6)):
                pool.memset(pool_c[:, n, :], value).then_inc(prep_pool, 1)
            pool.wait_ge(prep_pool, 3)
            with pool.Fori(0, NB) as i:
                made = [0]

                def link(ins):
                    made[0] += 1
                    ins.then_inc(pool_link.sem, 1)
                    pool.wait_ge(pool_link.sem, pool_link.at(i, made[0]))

                def rstd(n, var, dst, eps, width):
                    if n == 1:
                        await_drained(pool, i, "gn_var")
                    else:
                        pool.wait_ge(stats_ready.sem, stats_ready.at(i, n + (n == 0)))
                    link(pool.tensor_tensor(dst, var, eps, ALU.add))
                    pool.tensor_tensor(dst, dst, pool_c[:, 0, 0:width], ALU.pow).then_inc(rstd_ready.sem, 1)

                def residual(n, extra, bias):
                    if extra is not None:
                        link(pool.tensor_tensor(h[:, :, :], h[:, :, :], extra, ALU.add))
                    pool.tensor_tensor(h[:, :, :], h[:, :, :], bias.unsqueeze(1).broadcast_to([P, T, C]), ALU.add)\
                        .then_inc(res_ready.sem, 1)

                def normalize(layer, D):
                    for u in range(16):
                        head, g = u // 2, u % 2
                        for jj in range(2):
                            n = 32 * layer + 2 * u + jj
                            t = 4 * g + 2 * jj
                            pool.wait_ge(o_drained.sem, o_drained.at(i, n + 1))
                            o = on[:, t:t + 2, head * D:(head + 1) * D]
                            pool.tensor_tensor(o, o, o_r[:, n % 4, :].unsqueeze(2).broadcast_to([P, 2, D]), ALU.mult)\
                                .then_inc(on_ready.sem, 1)

                rstd(0, mv[:, :, 1], rs[:, :], pool_c[:, 1, :], T)
                rstd(1, gsm[:, 4:5], gsm[:, 5:6], pool_c[:, 2, 0:1], 1)
                pool.wait_ge(z_ready.sem, z_ready.at(i, 2))
                residual(0, z[:, :, :], bo_b[:, :])
                normalize(0, D0)
                rstd(2, mv[:, :, 1], rs[:, :], pool_c[:, 1, :], T)
                pool.wait_ge(z_ready.sem, z_ready.at(i, 4))
                residual(1, None, b2_b[:, :])
                rstd(3, mv[:, :, 1], rs[:, :], pool_c[:, 1, :], T)
                pool.wait_ge(z_ready.sem, z_ready.at(i, 6))
                residual(2, None, bo1_b[:, :])
                normalize(1, D1)
                rstd(4, mv[:, :, 1], rs[:, :], pool_c[:, 1, :], T)
                await_drained(pool, i, "rank")
                for t in range(1, T):
                    pool.tensor_tensor(prefix[:, t, :], prefix[:, t - 1, :], oh[:, t - 1, :], ALU.add)\
                        .then_inc(prefix_ready.sem, 1)
                    pool.wait_ge(prefix_ready.sem, prefix_ready.at(i, t))
                await_drained(pool, i, "e6.3", "e7.3")
                pool.dma_start(out_v[i], h[:, :, :]).then_inc(out_stored.sem, 16)
                pool.wait_ge(out_stored.sem, out_stored.at(i, 16))
                pool.sem_inc(h_free.sem, 1)
                assert made[0] == POOL_LINKS, made

        @block.vector
        def _(dve):
            dve.memset(ones[:, :], 1.0).then_inc(prep_dve, 1)
            dve.memset(kB[64:65, :, :].bitcast(F32), 1.0)
            dve.memset(v0[:, :, :, 2 * D0:2 * D0 + 2], 1.0)
            dve.memset(v1[:, :, :, 2 * D1:2 * D1 + 2], 1.0)
            dve.memset(seen[:, :], 0.0)
            dve.wait_ge(load_small, 16 * N_SMALL)
            for n in range(2):
                last = dve.tensor_tensor(pr[:, 1, 0, n * P:(n + 1) * P], pr[:, 0, 0, n * P:(n + 1) * P], lower, ALU.mult)
            last.then_inc(prep_dve, 1)
            dve.wait_ge(prep_dve, 2)
            for c in range(NCH):
                last = dve.tensor_scalar(pr[:, 1, 1, c * P:(c + 1) * P], ones[:, :], bv_c[:, c:c + 1], None, ALU.mult)
            last.then_inc(prep_dve, 1)
            dve.tensor_scalar(pr[:, 1, 2, 0:P], ones[:, :], bv1_c, None, ALU.mult).then_inc(prep_dve, 1)
            dve.wait_ge(prep_pe, 1)
            for n in range(4):
                dve.tensor_copy(ewT[:, 4 * n:4 * n + 4, :], banks[n][:, :].rearrange("p (e f) -> p e f", f=P))
            dve.tensor_copy(w1T[:, :], banks[4][:, 0:P])
            dve.tensor_copy(w2T[:, :], banks[4][:, P:2 * P])
            dve.tensor_copy(swT[:, :], banks[4][:, 2 * P:2 * P + E])
            dve.tensor_copy(bo_b[:, :], banks[5][:, 0:P])
            dve.tensor_copy(bo1_b[:, :], banks[6][:, 0:P])
            dve.tensor_copy(b2_b[:, :], banks[7][:, 0:P])
            dve.tensor_copy(sb_b[:, :], banks[7][:, P:P + E]).then_inc(prep_dve, 1)
            dve.wait_ge(prep_dve, PREP_DVE)
            dve.sem_inc(glue_drained[0].sem, 1)
            dve.sem_inc(glue_drained[1].sem, 1)
            dve.sem_inc(max_reduced.sem, 2)
            dve.sem_inc(exp_done.sem, 2)
            dve.sem_inc(o_drained.sem, 2)
            dve.sem_inc(h_free.sem, 1)

            with dve.Fori(0, NB) as i:
                made = [0]

                def mark(ins):
                    made[0] += 1
                    ins.then_inc(dve_link.sem, 1)

                def settle(behind=0):
                    dve.wait_ge(dve_link.sem, dve_link.at(i, made[0] - behind))

                def link(ins):
                    mark(ins)
                    settle()

                def full(name):
                    b, k = plan[name]
                    dve.wait_ge(glue_filled[b].sem, glue_filled[b].at(i, k + 1))
                    return glue[b], glue_drained[b].sem

                def bank_tiles(bank):
                    return bank[:, :].rearrange("p (t c) -> p t c", t=4)

                def layer_norm(n):
                    for t in range(T):
                        ins = dve.bn_stats(st[:, t, :], h[:, t, :])
                    link(ins)
                    dve.memset(gsm[:, 7:8], 0.0)
                    for t in range(T):
                        ins = dve.bn_aggr(mv[:, t, :], st[:, t, :])
                    ins.then_inc(stats_ready.sem, 1)
                    k = n if n == 0 else n + 1
                    dve.wait_ge(stats_ready.sem, stats_ready.at(i, n + 1))
                    dve.wait_ge(rstd_ready.sem, rstd_ready.at(i, k + 1))
                    for g in range(2):
                        for j in range(4):
                            t = 4 * g + j
                            ins = dve.tensor_scalar(z[:, t, :], h[:, t, :], mv[:, t, 0:1], rs[:, t:t + 1],
                                                    ALU.subtract, ALU.mult)
                        ins.then_inc(z_ready.sem, 1)

                def add_result(name, res=None, base=None):
                    for g in range(2):
                        bank, drained = full(f"{name}{g}")
                        if res is not None and g == 0:
                            dve.wait_ge(res_ready.sem, res_ready.at(i, res))
                        src = (base if base is not None else h)[:, 4 * g:4 * g + 4, :]
                        dve.tensor_tensor(h[:, 4 * g:4 * g + 4, :], bank_tiles(bank), src, ALU.add).then_inc(drained, 1)
                    await_drained(dve, i, f"{name}0", f"{name}1")

                dve.wait_ge(h_free.sem, h_free.at(i, 0))
                add_result("h", base=pe_sb)
                layer_norm(0)
                await_drained(dve, i, "zT0.0", "zT0.1")
                for g in range(2):
                    ins = dve.bn_stats(gst[:, g, :], zT[:, g * HALF:(g + 1) * HALF])
                link(ins)
                dve.memset(gsm[:, 7:8], 0.0)
                link(dve.bn_aggr(gmv[:, :], gst[:, :, :].rearrange("p a b -> p (a b)")))
                dve.tensor_copy(gsm[:, 0:1], gmv[:, 0:1]).then_inc(gn_stat.sem, 1)
                bank, drained = full("gn_mean")
                dve.tensor_copy(gsm[:, 2:3], bank[:, 0:1]).then_inc(drained, 1)
                await_drained(dve, i, "gn_mean")
                link(dve.tensor_tensor(gsm[:, 3:4], gmv[:, 0:1], gsm[:, 2:3], ALU.subtract))
                dve.scalar_tensor_tensor(gsm[:, 1:2], gsm[:, 3:4], gsm[:, 3:4], gmv[:, 1:2], ALU.mult, ALU.add)\
                    .then_inc(gn_stat.sem, 1)
                bank, drained = full("gn_var")
                dve.tensor_copy(gsm[:, 4:5], bank[:, 0:1]).then_inc(drained, 1)
                dve.wait_ge(rstd_ready.sem, rstd_ready.at(i, 2))
                link(dve.tensor_tensor(gsm[:, 6:7], gsm[:, 5:6], gnw_c, ALU.mult))
                link(dve.tensor_tensor(gsm[:, 3:4], gsm[:, 2:3], gsm[:, 6:7], ALU.mult))
                link(dve.tensor_tensor(gsm[:, 7:8], gnb_c, gsm[:, 3:4], ALU.subtract))
                dve.tensor_scalar(zT[:, :], zT[:, :], gsm[:, 6:7], gsm[:, 7:8], ALU.mult, ALU.add).then_inc(xn_ready.sem, 1)
                for t in range(T):
                    bank, drained = full(f"v0.{t}")
                    dve.wait_ge(parts_hi.sem, parts_hi.at(i, t + 1))
                    dve.tensor_tensor(v0[:, t, :, D0:2 * D0], bank[:, :].rearrange("p (h d) -> p h d", d=D0),
                                      v0[:, t, :, 0:D0], ALU.subtract).then_inc(drained, 1)

                def lo_part(name, hi_count, hi, lo, g, bias):
                    bank, drained = full(name)
                    dve.wait_ge(parts_hi.sem, parts_hi.at(i, hi_count))
                    sl = slice(g * HALF, (g + 1) * HALF)
                    dve.scalar_tensor_tensor(lo[:, sl], bank[:, :], bias, hi[:, sl].bitcast(F32), ALU.add, ALU.subtract)\
                        .then_inc(drained, 1)

                def project(c):
                    for w, (hi, lo, bias) in enumerate(((q_hi, q_lo, bq_c), (k_hi, k_lo, bk_c))):
                        for g in range(2):
                            n = 4 * c + 2 * w + g + 1
                            lo_part(QK0["qk"[w], c, g], 8 + n, hi[:, 0], lo[:, 0], g, bias[:, c:c + 1])

                def max_tile(layer, head, n):
                    k = 128 * layer + 16 * head + n
                    dve.wait_ge(max_filled.sem, max_filled.at(i, k + 1))
                    dve.tensor_reduce(mxh[:, head % 2, n // 2, n % 2:n % 2 + 1], maxb[k % 2][:, :], AX_X, ALU.max)\
                        .then_inc(max_reduced.sem, 1)

                def max_all(layer, head):
                    dve.wait_ge(max_reduced.sem, max_reduced.at(i, 128 * layer + 16 * head + 16))
                    dve.tensor_reduce(mx[:, head % 2, :], mxh[:, head % 2, :, :], AX_X, ALU.max).then_inc(max_ready.sem, 1)

                def lo_pair(layer, head, g, kt):
                    u = 2 * head + g
                    k = 128 * layer + 16 * head + 8 * g + kt
                    dve.wait_ge(exp_done.sem, exp_done.at(i, k + 1))
                    w = pr[:, u % 2, kt - 1:kt + 1, :].rearrange("p a b -> p (a b)")
                    hi = w.bitcast(BF16).rearrange("p (q two) -> p q two", two=2)[:, :, 1]
                    dve.tensor_tensor(pr_lo[:, u % 2, kt - 1:kt + 1, :].rearrange("p a b -> p (a b)"), w, hi, ALU.subtract)\
                        .then_inc(lo_done.sem, 1)

                def outputs(layer, u, jj, D):
                    n = 32 * layer + 2 * u + jj
                    head, t = u // 2, 4 * (u % 2) + 2 * jj
                    dve.wait_ge(o_hi_out.sem, o_hi_out.at(i, n + 1))
                    bank = obank[n % 2][:, :].rearrange("p (j n) -> p j n", j=2)
                    if n >= 4:
                        dve.wait_ge(on_ready.sem, on_ready.at(i, n - 3))
                    dve.reciprocal(o_r[:, n % 4, :], bank[:, :, 2 * D])
                    dve.tensor_tensor(on[:, t:t + 2, head * D:(head + 1) * D], bank[:, :, D:2 * D],
                                      o_hi[:, n % 2, :, 0:D], ALU.add).then_inc(o_drained.sem, 1)

                def attention(layer):
                    D = D0 if layer == 0 else D1
                    for n in range(16):
                        max_tile(layer, 0, n)
                    max_all(layer, 0)
                    for head in range(8):
                        for g in range(2):
                            u = 2 * head + g
                            for kt in range(T):
                                step = 8 * g + kt
                                if head < 7:
                                    for n in MAX_STEPS[step]:
                                        max_tile(layer, head + 1, n)
                                    if MAX_STEPS[step] and MAX_STEPS[step][-1] == 15:
                                        max_all(layer, head + 1)
                                if kt % 2 == 1:
                                    lo_pair(layer, head, g, kt)
                                if u >= 1 and kt % 4 == 3:
                                    outputs(layer, u - 1, kt // 4, D)
                        if layer == 0 and head % 2 == 0 and head < 6:
                            project(head // 2 + 1)
                    for jj in range(2):
                        outputs(layer, 15, jj, D)

                project(0)
                attention(0)
                add_result("attn0.", res=1)
                layer_norm(1)
                add_result("ffn_o", res=2)
                layer_norm(2)
                for w, (hi, lo, bias) in enumerate(((q_hi, q_lo, bq1_c), (k_hi, k_lo, bk1_c))):
                    for g in range(2):
                        n = 16 + 2 * w + g + 1
                        lo_part(QK1["qk"[w], g], 8 + n, hi[:, 1], lo[:, 1], g, bias)
                for g in range(2):
                    bank, drained = full(f"v1.{g}")
                    dve.wait_ge(parts_hi.sem, parts_hi.at(i, 29 + g))
                    v = v1[:, 4 * g:4 * g + 4, :, :]
                    src = bank[:, :].rearrange("p (t h d) -> p t h d", t=4, d=D1)
                    dve.tensor_tensor(v[:, :, :, D1:2 * D1], src, v[:, :, :, 0:D1], ALU.subtract).then_inc(drained, 1)
                attention(1)
                add_result("attn1.", res=3)
                layer_norm(3)
                def over_e(a):
                    return a.unsqueeze(2).broadcast_to([P, T, E])
                top, total, rp, vm, pos, kr, un = (small[:, n, :] for n in range(7))
                bank, drained = full("logits")
                dve.tensor_tensor(lg[:, :, :], bank[:, 0:T * E].rearrange("p (t e) -> p t e", e=E),
                                  sb_b[:, :].unsqueeze(1).broadcast_to([P, T, E]), ALU.add).then_inc(drained, 1)
                await_drained(dve, i, "logits")
                link(dve.tensor_reduce(top, lg[:, :, :], AX_X, ALU.max))
                dve.tensor_tensor(ex[:, :, :], lg[:, :, :], over_e(top), ALU.subtract).then_inc(logit_ready.sem, 1)
                link(dve.tensor_tensor(oh[:, :, :], lg[:, :, :], over_e(top), ALU.is_equal))
                link(dve.tensor_tensor(lg[:, :, :], oh[:, :, :], desc.rearrange("p (t e) -> p t e", e=E), ALU.mult))
                link(dve.tensor_reduce(vm, lg[:, :, :], AX_X, ALU.max))
                link(dve.tensor_tensor(oh[:, :, :], lg[:, :, :], over_e(vm), ALU.is_equal))
                dve.tensor_reduce(per_p[:, :], oh[:, :, :].rearrange("p t e -> p e t"), AX_X, ALU.add).then_inc(oh_ready.sem, 1)
                dve.wait_ge(ex_ready.sem, ex_ready.at(i, 1))
                link(dve.tensor_reduce(total, ex[:, :, :], AX_X, ALU.add))
                link(dve.reciprocal(rp, total))
                bank, drained = full("rank")
                link(dve.tensor_tensor(prefix[:, 0, :], bank[:, 0:E], seen[:, :], ALU.add))
                dve.tensor_tensor(seen[:, :], bank[:, E:2 * E], seen[:, :], ALU.add).then_inc(drained, 1)
                dve.wait_ge(prefix_ready.sem, prefix_ready.at(i, 7))
                link(dve.tensor_tensor(lg[:, :, :], oh[:, :, :], prefix[:, :, :], ALU.mult))
                link(dve.tensor_reduce(pos, lg[:, :, :], AX_X, ALU.add))
                link(dve.scalar_tensor_tensor(kr, pos, CAP, rp, ALU.is_lt, ALU.mult))
                link(dve.tensor_tensor(un, rp, kr, ALU.subtract))
                dve.tensor_tensor(wgt[:, :, :], oh[:, :, :], over_e(kr), ALU.mult).then_inc(wgt_ready.sem, 1)
                for t in range(T):
                    ins = dve.scalar_tensor_tensor(h[:, t, :], z[:, t, :], un[:, t:t + 1], h[:, t, :], ALU.mult, ALU.add)
                link(ins)
                for g in range(2):
                    bank, drained = full(f"eb{g}")
                    dve.tensor_tensor(h[:, 4 * g:4 * g + 4, :], bank_tiles(bank), h[:, 4 * g:4 * g + 4, :], ALU.add)\
                        .then_inc(drained, 1)
                await_drained(dve, i, "eb0", "eb1")
                for t0 in range(0, T, 2):
                    for q in range(4):
                        both = [full(f"e{t0 + d}.{q}") for d in range(2)]
                        for e in range(4):
                            for d in range(2):
                                t, (bank, drained) = t0 + d, both[d]
                                if e > 0:
                                    settle(0 if (e, d) == (3, 1) else 1)
                                elif q > 0:
                                    await_drained(dve, i, f"e{t}.{q - 1}")
                                ins = dve.scalar_tensor_tensor(h[:, t, :], bank[:, e * P:(e + 1) * P],
                                                               wgt[:, t, 4 * q + e:4 * q + e + 1], h[:, t, :], ALU.mult, ALU.add)
                                if e < 3:
                                    mark(ins)
                                else:
                                    ins.then_inc(drained, 1)
                if "pad" in plan:
                    bank, drained = full("pad")
                    dve.tensor_copy(gsm[:, 3:4], bank[:, 0:1]).then_inc(drained, 1)
                assert made[0] == DVE_LINKS, made


MAX_STEPS = {s: [] for s in range(16)}
for _n in range(16):
    MAX_STEPS[4 + (_n * 10) // 16].append(_n)
N_SMALL = 29
PREP_DVE = 5
DVE_LINKS = 119
POOL_LINKS = 6

_INS = ['x', 'L0_tok_W', 'L0_attn_gn_w', 'L0_attn_gn_b', 'L0_attn_wq', 'L0_attn_bq', 'L0_attn_wk', 'L0_attn_bk',
        'L0_attn_wv', 'L0_attn_bv', 'L0_attn_wo', 'L0_attn_bo', 'L0_ffn_W1', 'L0_ffn_b1', 'L0_ffn_W2', 'L0_ffn_b2',
        'L1_attn_Wq', 'L1_attn_Wk', 'L1_attn_Wv', 'L1_attn_bq', 'L1_attn_bk', 'L1_attn_bv', 'L1_attn_Wo', 'L1_attn_bo',
        'L1_ffn_switch_w', 'L1_ffn_switch_b', 'L1_ffn_expert_w', 'L1_ffn_expert_b']


def shape_tables(S, C, E):
    position = np.arange(2 * S, dtype=np.float32)[:, None]
    div_term = np.exp(np.arange(0, C, 2, dtype=np.float32) * (-math.log(10000.0) / C))
    pe = np.zeros((2 * S, C), dtype=np.float32)
    pe[:, 0::2] = np.sin(position * div_term)
    pe[:, 1::2] = np.cos(position * div_term)
    r = np.arange(P)
    tri = np.stack([
        np.eye(P), (r[:, None] // 4 == r[None, :] // 4) / 4.0, r[:, None] < r[None, :], r[:, None] >= r[None, :],
        np.broadcast_to(E - (r % E), (P, P)),
    ], axis=1).astype(np.float32)
    return pe[:S].reshape(P, S // P, C), tri


def kernel(**inputs):
    import concourse.bacc as _bacc
    from concourse.bass_utils import run_bass_kernel_spmd as _run

    nc = _bacc.Bacc("TRN2", target_bir_lowering=False, num_devices=1)
    arrays, args = {}, []
    for name in _INS:
        a = np.ascontiguousarray(inputs[name])
        arrays[f"in_{name}"] = a
        args.append(nc.dram_tensor(f"in_{name}", a.shape, mybir.dt.from_np(a.dtype), kind="ExternalInput").ap())
    for name, a in zip(("pe", "tri"), shape_tables(1024, 128, 16)):
        a = np.ascontiguousarray(a)
        arrays[f"in_{name}"] = a
        args.append(nc.dram_tensor(f"in_{name}", a.shape, mybir.dt.from_np(a.dtype), kind="ExternalInput").ap())
    nb = inputs["x"].shape[0]
    out = nc.dram_tensor("out_0", (nb, 1024, 128), F32, kind="ExternalOutput").ap()
    build(nc, *args, out)
    r = _run(nc, [arrays], core_ids=[0])
    return r.results[0]["out_0"]
```

```python
from contextlib import ExitStack
import math

import numpy as np

import concourse.bass as bass
from concourse import mybir

F32 = mybir.dt.float32
F32R = mybir.dt.float32r
BF16 = mybir.dt.bfloat16
ALU = mybir.AluOpType
ACT = mybir.ActivationFunctionType
AX_X = mybir.AxisListType.X

P = 128


EMBED_SLOTS = {"xT0": 3, "xT1": 4, "h0": 6, "h1": 7, "ln": 9, "z": 13, "zT0.0": 15, "zT0.1": 16, "gn": 19,
               "gn_mean": 21, "gn_var": 24, "xn": 27, **{f"v0.{t}": 32 + t for t in range(8)},
               **{f"{w}0.{g}": 104 + n for n, (w, g) in enumerate((w, g) for w in "qk" for g in range(2))}}
SWITCH_SLOTS = {"oT1.0": 11, "oT1.1": 12, "attn1.0": 14, "attn1.1": 15, "ln": 20, "z": 26, "zT3.0": 29, "zT3.1": 30,
                "logits": 46, "route": 50, "rank": 53, "place": 58, "wT0": 62, "wT1": 63, "eb0": 66, "eb1": 67,
                **{f"e{n}.{d}": slot for n, slot in enumerate((69, 81, 86, 89, 94, 97, 102, 105)) for d in range(2)}}
EXPERT_SLOTS = [117, 119, 122, 125, "start", "ln1", "ln2", "max"]
MLP_SLOTS = {name: 128 + n for n, name in enumerate((
    "start", "oT0.3.0", "oT0.3.1", "attn0.0", "attn0.1", "ln1", "zT1.0", "zT1.1", "ffn_h0", "ffn_h1", "ffn_o0", "ffn_o1",
    "ln2", "zT2.0", "zT2.1", "q1.L1.0", "q1.L1.1", "k1.L1.0", "k1.L1.1", "v1.0", "v1.1", "max", "m1.0.0"))}
EXPERT_SLOTS = [MLP_SLOTS.get(slot, slot) for slot in EXPERT_SLOTS]
PROJECT_SLOTS = {f"{w}{c}.{g}": 32 * (c - 1) + 7 + 2 * (w == "k") + g for c in range(1, 4) for w in "qk" for g in range(2)}
TURN_SLOTS = {f"oT0.{c}.{g}": 32 * (c + 1) + 12 + g for c in range(3) for g in range(2)}

def max_tile_step(layer, n):
    return n - (12, 13)[layer]


ROW_STEPS = ((-4, 4), (-5, 3))


def glue_plan(kind):
    def ordered(*tables):
        items = [(slot, n, name) for n, table in enumerate(tables) for name, slot in table.items()
                 if name not in ("ln", "z", "gn", "xn", "route", "place", "start", "ln1", "ln2", "max")]
        return [name for _, _, name in sorted(items, key=lambda it: it[:2])]

    def rows(layer, next_head=None):
        at = {f"m{layer}.{h}.{g}": 16 * h + ROW_STEPS[layer][g] for h in range(8) for g in range(2) if (h, g) != (0, 0)}
        return {**at, next_head: 128 + ROW_STEPS[0][0]} if next_head else at

    uses = []
    if kind == "first":
        uses += ordered(EMBED_SLOTS) + ["m0.0.0"]
    elif kind == "loop":
        uses += ordered(rows(1, "m0.0.0"), EMBED_SLOTS)
    else:
        uses += ordered(rows(1)) + ordered(SWITCH_SLOTS)
    if kind != "last":
        uses += ordered({**rows(0), **PROJECT_SLOTS, **TURN_SLOTS}, SWITCH_SLOTS if kind == "loop" else {})
        uses += ordered(MLP_SLOTS)
    assert len(set(uses)) == len(uses)
    return {u: (n % 2, n // 2) for n, u in enumerate(uses)}, ((len(uses) + 1) // 2, len(uses) // 2)


class Batch:

    def __init__(self, turn, ahead=0):
        self.turn, self.ahead = turn, ahead

    def times(self, per, count):
        if isinstance(self.turn, int):
            return (self.turn + self.ahead) * per + count
        return self.turn * per + (self.ahead * per + count)

    def index(self):
        return self.turn + self.ahead if self.ahead else self.turn


class Segment:

    def __init__(self, kind, turn, nb):
        self.kind, self.turn, self.nb = kind, turn, nb
        self.old = {"first": None, "loop": Batch(turn), "last": Batch(nb - 1)}[kind]
        self.new = {"first": Batch(0), "loop": Batch(turn, 1), "last": None}[kind]
        self.made = 0

    def after(self, first, loop, count):
        if self.kind == "first":
            return count
        if self.kind == "loop":
            return self.turn * loop + (first + count)
        return first + (self.nb - 1) * loop + count


class Counts:

    def __init__(self, sem, per_batch, credit=0):
        self.sem, self.per_batch, self.credit = sem, per_batch, credit

    def at(self, batch, count):
        return batch.times(self.per_batch, count + self.credit)


class Beside:

    def __init__(self, steps):
        self.steps = steps
        self.due = next(steps, None)

    def run(self, slot):
        while self.due is not None and self.due <= slot:
            self.due = next(self.steps, None)


def build(nc, x, tok_w, gn_w, gn_b, wq, bq, wk, bk, wv, bv, wo, bo, w1, b1, w2, b2,
          wq1, wk1, wv1, bq1, bk1, bv1, wo1, bo1, sw, sb_, ew, eb, pe, tri, out):
    NB, HH, WW, FT = x.shape
    S = HH * WW
    T = S // P
    C = tok_w.shape[1]
    H0, D0 = 8, 64
    H1, D1 = wq1.shape[0], wq1.shape[2]
    E = sw.shape[0]
    CAP = float(int(1.2 * (NB * S) / E))
    INNER = H0 * D0
    NCH = INNER // P
    HALF = S // 2
    assert C == P and T == 8 and D0 == 64 and H1 * D1 == P and E * T == P

    with ExitStack() as ctx:
        def sb(name, shape, dt=F32):
            return ctx.enter_context(nc.sbuf_tensor(name, shape, dt))

        def sem(name):
            return ctx.enter_context(nc.semaphore(name))

        tri_sb = sb("tri_sb", [P, 5, P])
        ident, group4, before, lower, desc = (tri_sb[:, n, :] for n in range(5))
        ones = sb("ones", [P, P])
        pool_c = sb("pool_c", [P, 3, T])
        pe_sb = sb("pe_sb", [P, T, C])
        tokw_sb = sb("tokw_sb", [FT, C])
        wq_sb = sb("wq_sb", [P, INNER])
        wk_sb = sb("wk_sb", [P, INNER])
        wv_sb = sb("wv_sb", [P, INNER])
        wo_sb = sb("wo_sb", [P, NCH, C])
        w1T = sb("w1T", [P, P])
        w2T = sb("w2T", [P, P])
        wq1_sb = sb("wq1_sb", [P, P])
        wk1_sb = sb("wk1_sb", [P, P])
        wv1_sb = sb("wv1_sb", [P, P])
        wo1_sb = sb("wo1_sb", [P, P])
        swT = sb("swT", [P, E])
        ewT = sb("ewT", [P, E, P])
        eb_sb = sb("eb_sb", [E, P])
        cols = sb("cols", [P, 24])
        gnw_c, gnb_c, b1_c, bq1_c, bk1_c = (cols[:, n:n + 1] for n in range(5))
        bq_c, bk_c, bv_c, bv1_c = cols[:, 5:9], cols[:, 9:13], cols[:, 13:17], cols[:, 17:18]
        rows = sb("rows", [1, 4 * P])
        bo_b = sb("bo_b", [P, C])
        b2_b = sb("b2_b", [P, C])
        bo1_b = sb("bo1_b", [P, C])
        sb_b = sb("sb_b", [P, E])

        xin = sb("xin", [P, T, FT])
        h0 = sb("h0", [P, T, C])
        h = sb("h", [P, T, C])
        hm = sb("hm", [P, T, C])
        z = sb("z", [P, T, C])
        zT = sb("zT", [P, S])
        mT = sb("mT", [P, S])
        xnT = sb("xnT", [P, S])
        xT = sb("xT", [P, S])
        st = sb("st", [P, T, 6])
        mv = sb("mv", [P, T, 2])
        rs = sb("rs", [P, T])
        gst = sb("gst", [P, 2, 6])
        gmv = sb("gmv", [P, 2])
        gsm = sb("gsm", [P, 8])
        v0 = sb("v0", [P, T, H0, 2 * D0 + 2], BF16)
        v1 = sb("v1", [P, T, H1, 2 * D1 + 2], BF16)
        parts = sb("parts", [P, 4, S], F32R)
        k_lo, k_hi, q_hi, q_lo = (parts[:, n, :] for n in range(4))
        stacks = sb("stacks", [P, 2, 4, S], F32R)
        kB, kA, qA, qB = (stacks[:, :, n, :] for n in range(4))
        pr = sb("pr", [P, 2, T, HALF])
        pr_lo = sb("pr_lo", [P, 2, T, HALF], BF16)
        mxh = sb("mxh", [P, 2, T, 2])
        mx = sb("mx", [P, 2, T])
        mrow = sb("mrow", [T // 2, 4, P], F32R)
        o_hi = sb("o_hi", [P, 2, 2, D0])
        o_r = sb("o_r", [P, 4, 2])
        on = sb("on", [P, T, INNER])
        on1 = sb("on1", [P, T, P])
        lg = sb("lg", [P, T, E])
        ex = sb("ex", [P, T, E])
        oh = sb("oh", [P, T, E])
        prefix = sb("prefix", [P, T, E])
        wgt = sb("wgt", [P, T, E])
        small = sb("small", [P, 8, T])
        seen = sb("seen", [P, E])
        per_p = sb("per_p", [P, E])

        banks = [ctx.enter_context(nc.psum_tensor(f"bank{n}", [P, 512], F32)) for n in range(8)]
        glue, score, maxb, obank = banks[0:2], banks[2:4], banks[4:6], banks[6:8]

        plans = {kind: glue_plan(kind) for kind in ("first", "loop", "last")}
        load_small = sem("load_small")
        prep_pe = sem("prep_pe")
        prep_dve = sem("prep_dve")
        prep_pool = sem("prep_pool")
        x_loaded = Counts(sem("x_loaded"), 16)
        out_stored = Counts(sem("out_stored"), 16)
        hm_free = Counts(sem("hm_free"), 1, credit=1)
        expert_filled = Counts(sem("expert_filled"), 8)
        expert_drained = Counts(sem("expert_drained"), 8)
        glue_filled = [sem(f"glue_filled{b}") for b in range(2)]
        glue_drained = [sem(f"glue_drained{b}") for b in range(2)]
        z_ready = [Counts(sem(f"z_ready{n}"), 2) for n in range(4)]
        stats_ready = [Counts(sem(f"stats_ready{n}"), 1) for n in range(4)]
        rstd_ready = [Counts(sem(f"rstd_ready{n}"), 1) for n in range(5)]
        gn_stat = Counts(sem("gn_stat"), 2)
        xn_ready = Counts(sem("xn_ready"), 1)
        parts_hi = Counts(sem("parts_hi"), 8 + 16 + 4 + 2)
        stacks0_in = [Counts(sem(f"stacks0_in{n}"), 16 * 3 * 4) for n in range(2)]
        stacks1_in = [Counts(sem(f"stacks1_in{n}"), 16 * 4 * 2) for n in range(4)]
        max_filled = Counts(sem("max_filled"), 256)
        max_reduced = Counts(sem("max_reduced"), 256, credit=2)
        max_ready = Counts(sem("max_ready"), 32)
        mrow_in = [Counts(sem(f"mrow_in{n}"), 16 * 8) for n in range(4)]
        score_filled = Counts(sem("score_filled"), 256)
        exp_done = Counts(sem("exp_done"), 256, credit=2)
        lo_done = Counts(sem("lo_done"), 32 * (4 - len(POOL_PAIRS)))
        lo_pool = Counts(sem("lo_pool"), 32 * len(POOL_PAIRS))
        o_filled = Counts(sem("o_filled"), 64)
        o_hi_out = Counts(sem("o_hi_out"), 64)
        o_drained = Counts(sem("o_drained"), 64, credit=2)
        on_ready = Counts(sem("on_ready"), 64)
        res_ready = Counts(sem("res_ready"), 3)
        logit_ready = Counts(sem("logit_ready"), 1)
        ex_ready = Counts(sem("ex_ready"), 1)
        oh_ready = Counts(sem("oh_ready"), 1)
        prefix_ready = Counts(sem("prefix_ready"), 7)
        wgt_ready = Counts(sem("wgt_ready"), 1)
        dve_link = sem("dve_link")
        pool_link = sem("pool_link")

        x_v = x.rearrange("b h w f -> b (h w) f").rearrange("b (p t) f -> b p t f", t=T)
        out_v = out.rearrange("b (p t) c -> b p t c", t=T)

        def glue_value(seg, name, uses, credit):
            b, k = plans[seg.kind][0][name]
            return b, seg.after(plans["first"][1][b], plans["loop"][1][b], k + uses + credit)

        def await_drained(eng, seg, *names):
            plan = plans[seg.kind][0]
            for b in range(2):
                uses = [(plan[name][1], name) for name in names if plan[name][0] == b]
                if uses:
                    eng.wait_ge(glue_drained[b], glue_value(seg, max(uses)[1], 1, 1)[1])

        def await_filled(eng, seg, name):
            b, value = glue_value(seg, name, 1, 0)
            eng.wait_ge(glue_filled[b], value)
            return glue[b], glue_drained[b]

        QK0 = {(w, c, g): f"{w}{c}.{g}" for w in "qk" for c in range(NCH) for g in range(2)}
        QK1 = {(w, g): f"{w}1.L1.{g}" for w in "qk" for g in range(2)}

        def heads_T(c):
            return (zT, xT, xnT, parts[:, 0, :].bitcast(F32))[c]

        block = ctx.enter_context(nc.Block())

        def lo_parts(eng, b, layer, u, kt):
            eng.wait_ge(exp_done.sem, exp_done.at(b, 128 * layer + 8 * u + kt + 1))
            w = pr[:, u % 2, kt - 1:kt + 1, :].rearrange("p a b -> p (a b)")
            hi = w.bitcast(BF16).rearrange("p (q two) -> p q two", two=2)[:, :, 1]
            return eng.tensor_tensor(pr_lo[:, u % 2, kt - 1:kt + 1, :].rearrange("p a b -> p (a b)"), w, hi, ALU.subtract)

        HALVES = [(w, g) for w in "qk" for g in range(2)]

        def steps_of(b, layer, before_unit, next_head):
            for head in range(8):
                for g in range(2):
                    u = 2 * head + g
                    unit = (b, layer, u - 1) if u >= 1 else before_unit
                    for kt in range(T):
                        step = 8 * g + kt
                        coming = [((b, layer, head), step)]
                        if head < 7 or next_head:
                            coming += [((b, layer, head + 1) if head < 7 else next_head, step - 16)]
                        tiles = [(*who, n) for who, at in coming for n in range(16) if max_tile_step(who[1], n) == at]
                        rows = [(*who, half) for who, at in coming for half in range(2) if ROW_STEPS[who[1]][half] == at]
                        yield head, g, kt, unit, tiles, rows

        EARLY_TILES = [[n for n in range(16) if max_tile_step(layer, n) < 0] for layer in range(2)]

        def k_stack(layer, head):
            return kB[:, head % 2] if layer == 0 else (kB, kA)[head % 2][:, head // 2 % 2]

        def q_stack(layer, head):
            return qB[:, head % 2] if layer == 0 else (qB, qA)[head % 2][:, head // 2 % 2]

        def stack_in(layer, head):
            return stacks0_in[head % 2] if layer == 0 else stacks1_in[head % 4]

        def await_stack(eng, b, layer, head):
            signal = stack_in(layer, head)
            eng.wait_ge(signal.sem, signal.at(b, 16 * (3 * (head // 2 + 1) if layer == 0 else 4 * (head // 4 + 1))))

        @block.sync
        def _(sp):
            small_loads = [
                (tri_sb[:, :, :], tri), (tokw_sb[:, :], tok_w), (wq_sb[:, :], wq), (wk_sb[:, :], wk), (wv_sb[:, :], wv),
                (pe_sb[:, :, :], pe), (wo_sb[:, :, :], wo.rearrange("(c p) n -> p c n", p=P)),
                (pr[:, 0, 0, 0:P], w1), (pr[:, 0, 0, P:2 * P], w2), (wo1_sb[:, :], wo1), (eb_sb[:, :], eb),
                (wq1_sb[:, :].rearrange("p (h e) -> p h e", e=D1), wq1.rearrange("h d e -> d h e")),
                (wk1_sb[:, :].rearrange("p (h e) -> p h e", e=D1), wk1.rearrange("h d e -> d h e")),
                (wv1_sb[:, :].rearrange("p (h e) -> p h e", e=D1), wv1.rearrange("h d e -> d h e")),
                (pr[0:E, 0, 1, 0:P], sw),
                (pr[:, 0, 2:6, :].rearrange("p a (e d) -> p (a e) d", d=P), ew.rearrange("e f d -> f e d")),
                (cols[:, 0:1], gn_w.rearrange("(p n) -> p n", n=1)), (cols[:, 1:2], gn_b.rearrange("(p n) -> p n", n=1)),
                (cols[:, 2:3], b1.rearrange("(p n) -> p n", n=1)),
                (cols[:, 3:4], bq1.rearrange("h e -> (h e)").rearrange("(p n) -> p n", n=1)),
                (cols[:, 4:5], bk1.rearrange("h e -> (h e)").rearrange("(p n) -> p n", n=1)),
                (cols[:, 5:9], bq.rearrange("(c p) -> p c", p=P)), (cols[:, 9:13], bk.rearrange("(c p) -> p c", p=P)),
                (cols[:, 13:17], bv.rearrange("(c p) -> p c", p=P)),
                (cols[:, 17:18], bv1.rearrange("h e -> (h e)").rearrange("(p n) -> p n", n=1)),
                (rows[:, 0:P], bo.rearrange("(a n) -> a n", a=1)), (rows[:, P:2 * P], b2.rearrange("(a n) -> a n", a=1)),
                (rows[:, 2 * P:3 * P], bo1.rearrange("(a n) -> a n", a=1)),
                (rows[:, 3 * P:3 * P + E], sb_.rearrange("(a n) -> a n", a=1)),
            ]
            assert len(small_loads) == N_SMALL
            with nc.allow_non_contiguous_dma(reason="a few biases as columns, once"):
                for dst, src in small_loads:
                    sp.dma_start(dst, src).then_inc(load_small, 16)
            slot_free = sp.alloc_register("slot_free")
            sp.wait_ge(prep_dve, PREP_DVE)

            def stack(seg, b, layer, head):
                s = head % 2 if layer == 0 else head // 2 % 2
                taken = layer == 1 or head >= 2 or seg.kind == "loop"
                if layer == 1:
                    sp.reg_mov(slot_free, score_filled.at(b, 16 * (head + 5 if head >= 4 else 7 + head // 2)))
                elif head >= 2:
                    sp.reg_mov(slot_free, score_filled.at(b, 16 * (head - 1)))
                elif taken:
                    sp.reg_mov(slot_free, score_filled.at(seg.old, 16 * (14 + 2 * head)))
                if layer == 0 or head == 0:
                    if not (layer == 0 and head % 2):
                        await_drained(sp, seg, QK0["k", head // 2, 1] if layer == 0 else QK1["k", 1])
                if taken:
                    sp.wait_ge(score_filled.sem, slot_free)
                if layer == 0:
                    a, b_ = D0 * s, D0 * s + D0
                    moves = [(stacks[0:D0, s, 0:2, :], k_hi[a:b_].unsqueeze(1).broadcast_to([D0, 2, S])),
                             (stacks[0:D0, s, 2:4, :], parts[a:b_, 2:4, :]),
                             (stacks[D0:P, s, 1:3, :], parts[a:b_, 0:4:2, :])]
                else:
                    a, b_ = D1 * head, D1 * head + D1
                    moves = []
                    for j in range(2):
                        r = slice(2 * D1 * j, 2 * D1 * (j + 1))
                        moves += [(k_stack(1, head)[r], parts[a:b_, 0:2, :]),
                                  (q_stack(1, head)[r], parts[a:b_, 2 + j, :].unsqueeze(1).broadcast_to([D1, 2, S]))]
                for dst, src in moves:
                    sp.dma_start(dst.bitcast(F32), src.bitcast(F32)).then_inc(stack_in(layer, head).sem, 16)

            def row(seg, layer, head, g):
                n = 2 * (head % 2) + g
                await_drained(sp, seg, f"m{layer}.{head}.{g}")
                sp.dma_start(q_stack(layer, head)[64:65, g * HALF:(g + 1) * HALF].rearrange("a (t q) -> a t q", t=T // 2).bitcast(F32),
                             mrow[:, n, :].bitcast(F32)).then_inc(mrow_in[n].sem, 16)

            def segment(seg):
                if seg.kind != "last":
                    sp.dma_start(xin[:, :, :], x_v[seg.new.index()]).then_inc(x_loaded.sem, 16)
                if seg.kind != "first":
                    for head in range(1, 8):
                        if head < 7:
                            stack(seg, seg.old, 1, head + 1)
                        row(seg, 1, head - 1, 1)
                        row(seg, 1, head, 0)
                if seg.kind != "last":
                    for head in range(8):
                        stack(seg, seg.new, 0, head)
                        if head > 0:
                            row(seg, 0, head - 1, 1)
                        elif seg.kind == "loop":
                            row(seg, 1, 7, 1)
                        row(seg, 0, head, 0)
                    row(seg, 0, 7, 1)
                    for head in range(2):
                        stack(seg, seg.new, 1, head)
                    row(seg, 1, 0, 0)
                else:
                    row(seg, 1, 7, 1)

            segment(Segment("first", 0, NB))
            with sp.Fori(0, NB - 1) as i:
                segment(Segment("loop", i, NB))
            segment(Segment("last", 0, NB))

        @block.tensor
        def _(te):
            mm = te.matmul
            te.wait_ge(load_small, 16 * N_SMALL)
            te.wait_ge(prep_dve, 4)
            for n in range(E):
                te.transpose(banks[n // 4][:, (n % 4) * P:(n % 4 + 1) * P],
                             pr[:, 0, 2 + n // 4, (n % 4) * P:(n % 4 + 1) * P], ident)
            te.transpose(banks[4][:, 0:P], pr[:, 1, 0, 0:P], ident)
            te.transpose(banks[4][:, P:2 * P], pr[:, 1, 0, P:2 * P], ident)
            te.transpose(banks[4][:, 2 * P:2 * P + E], pr[0:E, 0, 1, 0:P], ident[0:E, 0:E])
            for c in range(NCH):
                mm(banks[5][:, 0:P], pr[:, 1, 1, c * P:(c + 1) * P], wo_sb[:, c, :], start=(c == 0), stop=False)
            mm(banks[5][:, 0:P], ones[0:1, :], rows[:, 0:P], start=False, stop=True)
            mm(banks[6][:, 0:P], pr[:, 1, 2, 0:P], wo1_sb[:, :], start=True, stop=False)
            mm(banks[6][:, 0:P], ones[0:1, :], rows[:, 2 * P:3 * P], start=False, stop=True)
            mm(banks[7][:, 0:P], ones[0:1, :], rows[:, P:2 * P], start=True, stop=True)
            mm(banks[7][:, P:P + E], ones[0:1, :], rows[:, 3 * P:3 * P + E], start=True, stop=True).then_inc(prep_pe, 1)
            te.wait_ge(prep_dve, PREP_DVE)

            def use(seg, name):
                b, value = glue_value(seg, name, 0, 1)
                te.wait_ge(glue_drained[b], value)
                return glue[b], glue_filled[b]

            def turn(seg, name, src, rows_=P):
                bank, filled = use(seg, name)
                for j in range(4):
                    last = te.transpose(bank[0:rows_, j * P:(j + 1) * P], src(j), ident)
                last.then_inc(filled, 1)

            def z_turn(seg, b, n, g):
                te.wait_ge(z_ready[n].sem, z_ready[n].at(b, g + 1))
                turn(seg, f"zT{n}.{g}", lambda j: z[:, 4 * g + j, :])

            def project(seg, c, w, g):
                ws = wq_sb if w == "q" else wk_sb
                bank, filled = use(seg, QK0[w, c, g])
                mm(bank[:, :], ws[:, c * P:(c + 1) * P], xnT[:, g * HALF:(g + 1) * HALF],
                   start=True, stop=True).then_inc(filled, 1)

            def embed(seg):
                b, AT = seg.new, EMBED_SLOTS
                te.wait_ge(x_loaded.sem, x_loaded.at(b, 16))
                for g in range(2):
                    yield AT[f"xT{g}"]
                    turn(seg, f"xT{g}", lambda j: xin[:, 4 * g + j, :], FT)
                for g in range(2):
                    yield AT[f"h{g}"]
                    await_drained(te, seg, f"xT{g}")
                    bank, filled = use(seg, f"h{g}")
                    for j in range(4):
                        t = 4 * g + j
                        last = mm(bank[:, j * P:(j + 1) * P], xT[0:FT, t * P:(t + 1) * P], tokw_sb[:, :], start=True, stop=True)
                    last.then_inc(filled, 1)
                for g in range(2):
                    yield AT[f"zT0.{g}"]
                    z_turn(seg, b, 0, g)
                for n, name in enumerate(("gn_mean", "gn_var")):
                    yield AT[name]
                    te.wait_ge(gn_stat.sem, gn_stat.at(b, n + 1))
                    bank, filled = use(seg, name)
                    mm(bank[:, 0:1], group4, gsm[:, n:n + 1], start=True, stop=True).then_inc(filled, 1)
                for t in range(T):
                    yield AT[f"v0.{t}"]
                    if t == 0:
                        te.wait_ge(xn_ready.sem, xn_ready.at(b, 1))
                    bank, filled = use(seg, f"v0.{t}")
                    mm(bank[:, :], xnT[:, t * P:(t + 1) * P], wv_sb[:, :], start=True, stop=True).then_inc(filled, 1)
                for w, g in HALVES:
                    yield AT[QK0[w, 0, g]]
                    project(seg, 0, w, g)

            def more_heads(seg):
                for c in range(1, NCH):
                    for w, g in HALVES:
                        yield PROJECT_SLOTS[QK0[w, c, g]]
                        project(seg, c, w, g)

            def heads_turn(seg, c, g):
                te.wait_ge(on_ready.sem, on_ready.at(seg.new, 8 * (c + 1)))
                turn(seg, f"oT0.{c}.{g}", lambda j: on[:, 4 * g + j, c * P:(c + 1) * P])

            def done_heads(seg):
                for c in range(NCH - 1):
                    for g in range(2):
                        yield TURN_SLOTS[f"oT0.{c}.{g}"]
                        heads_turn(seg, c, g)

            def switch(seg):
                b, AT = seg.old, SWITCH_SLOTS
                for g in range(2):
                    yield AT[f"oT1.{g}"]
                    te.wait_ge(on_ready.sem, on_ready.at(b, 64))
                    turn(seg, f"oT1.{g}", lambda j: on1[:, 4 * g + j, :])
                for g in range(2):
                    yield AT[f"attn1.{g}"]
                    await_drained(te, seg, f"oT1.{g}")
                    bank, filled = use(seg, f"attn1.{g}")
                    for j in range(4):
                        last = mm(bank[:, j * P:(j + 1) * P], xT[:, (4 * g + j) * P:(4 * g + j + 1) * P], wo1_sb[:, :],
                                  start=True, stop=True)
                    last.then_inc(filled, 1)
                for g in range(2):
                    yield AT[f"zT3.{g}"]
                    z_turn(seg, b, 3, g)
                yield AT["logits"]
                await_drained(te, seg, "zT3.0", "zT3.1")
                bank, filled = use(seg, "logits")
                for t in range(T):
                    last = mm(bank[:, t * E:(t + 1) * E], mT[:, t * P:(t + 1) * P], swT[:, :], start=True, stop=True)
                last.then_inc(filled, 1)
                yield AT["rank"]
                te.wait_ge(oh_ready.sem, oh_ready.at(b, 1))
                bank, filled = use(seg, "rank")
                mm(bank[:, 0:E], before, per_p[:, :], start=True, stop=True)
                mm(bank[:, E:2 * E], ones[:, :], per_p[:, :], start=True, stop=True).then_inc(filled, 1)
                for g in range(2):
                    yield AT[f"wT{g}"]
                    te.wait_ge(wgt_ready.sem, wgt_ready.at(b, 1))
                    turn(seg, f"wT{g}", lambda j: wgt[:, 4 * g + j, :], E)
                for g in range(2):
                    yield AT[f"eb{g}"]
                    await_drained(te, seg, f"wT{g}")
                    bank, filled = use(seg, f"eb{g}")
                    for j in range(4):
                        t = 4 * g + j
                        last = mm(bank[:, j * P:(j + 1) * P], xT[0:E, t * P:(t + 1) * P], eb_sb[:, :], start=True, stop=True)
                    last.then_inc(filled, 1)
                def experts(dst, t, q):
                    return mm(dst[:, :], mT[:, t * P:(t + 1) * P], ewT[:, 4 * q:4 * q + 4, :].rearrange("p e f -> p (e f)"),
                              start=True, stop=True)

                for n in range(8):
                    yield AT[f"e{n}.0"]
                    for d in range(2):
                        bank, filled = use(seg, f"e{n}.{d}")
                        experts(bank, 2 * (n // 4) + d, n % 4).then_inc(filled, 1)
                for n, slot in enumerate(EXPERT_SLOTS):
                    yield slot
                    if n > 0:
                        te.wait_ge(expert_drained.sem, expert_drained.at(b, n))
                    elif seg.kind == "loop":
                        te.wait_ge(max_reduced.sem, max_reduced.at(seg.new, 128))
                    for d in range(2):
                        last = experts(maxb[d], 4 + 2 * (n // 4) + d, n % 4)
                    last.then_inc(expert_filled.sem, 1)

            def max_tile(b, layer, head, n):
                k = 128 * layer + 16 * head + n
                s, t, g = head % 2, n // 2, n % 2
                if n == 0:
                    await_stack(te, b, layer, head)
                te.wait_ge(max_reduced.sem, max_reduced.at(b, k - 1))
                if layer == 0:
                    qs, ks = qA[:, s], kA[:, s]
                else:
                    qs, ks = q_stack(1, head)[0:4 * D1], k_stack(1, head)[0:4 * D1]
                mm(maxb[k % 2][:, :], qs[:, t * P:(t + 1) * P], ks[:, g * HALF:(g + 1) * HALF],
                   start=True, stop=True).then_inc(max_filled.sem, 1)

            def max_turn(seg, b, layer, head, g):
                te.wait_ge(max_ready.sem, max_ready.at(b, 2 * (8 * layer + head) + g + 1))
                bank, filled = use(seg, f"m{layer}.{head}.{g}")
                te.transpose(bank[0:T // 2, 0:P], mx[:, head % 2, g * T // 2:(g + 1) * T // 2], ident).then_inc(filled, 1)

            def scores(b, layer, head, g, kt):
                k = 128 * layer + 16 * head + 8 * g + kt
                s = head % 2
                if kt == 0:
                    row = mrow_in[2 * s + g]
                    te.wait_ge(row.sem, row.at(b, 16 * (4 * layer + head // 2 + 1)))
                te.wait_ge(exp_done.sem, exp_done.at(b, k - 1))
                bank, q, kk = score[k % 2], slice(g * HALF, (g + 1) * HALF), slice(kt * P, (kt + 1) * P)
                if layer == 0:
                    mm(bank[:, :], kA[:, s, kk], qA[:, s, q], start=True, stop=False)
                mm(bank[:, :], k_stack(layer, head)[0:65, kk], q_stack(layer, head)[0:65, q], start=(layer == 1), stop=True).then_inc(score_filled.sem, 1)

            def values(b, layer, u, j):
                head = u // 2
                n = 32 * layer + 2 * u + j // 2
                v, w = (v0, 2 * D0 + 1) if layer == 0 else (v1, 2 * D1 + 1)
                if j == 0:
                    te.wait_ge(lo_done.sem, lo_done.at(b, (16 * layer + u + 1) * (4 - len(POOL_PAIRS))))
                    te.wait_ge(lo_pool.sem, lo_pool.at(b, (16 * layer + u + 1) * len(POOL_PAIRS)))
                if j % 2 == 0:
                    te.wait_ge(o_drained.sem, o_drained.at(b, n - 1))
                dst = obank[n % 2][:, (j % 2) * 256:(j % 2) * 256 + w]
                for kt in range(T):
                    hi = pr[:, u % 2, kt, j * P:(j + 1) * P].bitcast(BF16).rearrange("p (q two) -> p q two", two=2)[:, :, 1]
                    lo = pr_lo[:, u % 2, kt, j * P:(j + 1) * P]
                    mm(dst, hi, v[:, kt, head, 0:w], start=(kt == 0), stop=False)
                    last = mm(dst, lo, v[:, kt, head, 0:w], start=False, stop=(kt == T - 1))
                if j % 2 == 1:
                    last.then_inc(o_filled.sem, 1)

            def attention(seg, b, layer, before_unit, next_head, *beside):
                for head, g, kt, unit, tiles, rows in steps_of(b, layer, before_unit, next_head):
                    slot = 16 * head + 8 * g + kt
                    scores(b, layer, head, g, kt)
                    for tile in tiles:
                        max_tile(*tile)
                    if unit and kt in VALUE_STEPS:
                        if layer == 0 and slot == VALUE_STEPS[0] + 8:
                            await_drained(te, seg, "v0.6", "v0.7")
                        values(*unit, VALUE_STEPS.index(kt))
                    for row in rows:
                        max_turn(seg, *row)
                    for work in beside:
                        work.run(slot)

            def mlp(seg, *beside):
                b = seg.new

                def catch_up(name):
                    for work in beside:
                        work.run(MLP_SLOTS[name])

                catch_up("start")
                for j in range(4):
                    values(b, 0, 15, j)
                for g in range(2):
                    catch_up(f"oT0.3.{g}")
                    heads_turn(seg, 3, g)
                for g in range(2):
                    catch_up(f"attn0.{g}")
                    await_drained(te, seg, f"oT0.3.{g}", *(f"oT0.{c}.{g}" for c in range(NCH - 1)))
                    bank, filled = use(seg, f"attn0.{g}")
                    for j in range(4):
                        t = 4 * g + j
                        for c in range(NCH):
                            last = mm(bank[:, j * P:(j + 1) * P], heads_T(c)[:, t * P:(t + 1) * P], wo_sb[:, c, :],
                                      start=(c == 0), stop=(c == NCH - 1))
                    last.then_inc(filled, 1)
                catch_up("ln1")
                for g in range(2):
                    catch_up(f"zT1.{g}")
                    z_turn(seg, b, 1, g)
                for g in range(2):
                    catch_up(f"ffn_h{g}")
                    await_drained(te, seg, f"zT1.{g}")
                    bank, filled = use(seg, f"ffn_h{g}")
                    mm(bank[:, :], w1T[:, :], zT[:, g * HALF:(g + 1) * HALF], start=True, stop=True).then_inc(filled, 1)
                for g in range(2):
                    catch_up(f"ffn_o{g}")
                    await_drained(te, seg, f"ffn_h{g}")
                    bank, filled = use(seg, f"ffn_o{g}")
                    for j in range(4):
                        t = 4 * g + j
                        last = mm(bank[:, j * P:(j + 1) * P], xT[:, t * P:(t + 1) * P], w2T[:, :], start=True, stop=True)
                    last.then_inc(filled, 1)
                catch_up("ln2")
                for g in range(2):
                    catch_up(f"zT2.{g}")
                    z_turn(seg, b, 2, g)
                await_drained(te, seg, "zT2.0", "zT2.1")
                for w, g in HALVES:
                    catch_up(QK1[w, g])
                    bank, filled = use(seg, QK1[w, g])
                    mm(bank[:, :], (wq1_sb if w == "q" else wk1_sb)[:, :], zT[:, g * HALF:(g + 1) * HALF],
                       start=True, stop=True).then_inc(filled, 1)
                for g in range(2):
                    catch_up(f"v1.{g}")
                    bank, filled = use(seg, f"v1.{g}")
                    for j in range(4):
                        t = 4 * g + j
                        last = mm(bank[:, j * P:(j + 1) * P], zT[:, t * P:(t + 1) * P], wv1_sb[:, :], start=True, stop=True)
                    last.then_inc(filled, 1)
                catch_up("max")
                if seg.kind == "loop":
                    te.wait_ge(expert_drained.sem, expert_drained.at(seg.old, 8))
                for n in EARLY_TILES[1]:
                    max_tile(b, 1, 0, n)
                    if n == 7:
                        max_turn(seg, b, 1, 0, 0)
                await_drained(te, seg, "v1.0", "v1.1")

            def segment(seg):
                if seg.kind == "first":
                    Beside(embed(seg)).run(LAST_SLOT)
                    for n in EARLY_TILES[0]:
                        max_tile(seg.new, 0, 0, n)
                    max_turn(seg, seg.new, 0, 0, 0)
                    attention(seg, seg.new, 0, None, None, Beside(more_heads(seg)), Beside(done_heads(seg)))
                    mlp(seg)
                elif seg.kind == "loop":
                    attention(seg, seg.old, 1, None, (seg.new, 0, 0), Beside(embed(seg)))
                    switched = Beside(switch(seg))
                    attention(seg, seg.new, 0, (seg.old, 1, 15), None, Beside(more_heads(seg)), Beside(done_heads(seg)), switched)
                    mlp(seg, switched)
                else:
                    attention(seg, seg.old, 1, None, None)
                    for j in range(4):
                        values(seg.old, 1, 15, j)
                    Beside(switch(seg)).run(LAST_SLOT)

            segment(Segment("first", 0, NB))
            with te.Fori(0, NB - 1) as i:
                segment(Segment("loop", i, NB))
            segment(Segment("last", 0, NB))

        @block.scalar
        def _(act):
            def move_T(seg, name, dst, rows_=P):
                bank, drained = await_filled(act, seg, name)
                act.activation(dst, bank[0:rows_, :], ACT.Copy).then_inc(drained, 1)

            def project(seg, c, w, g):
                dst, bias = (q_hi, bq_c) if w == "q" else (k_hi, bk_c)
                bank, _ = await_filled(act, seg, QK0[w, c, g])
                if w == "q" and g == 0:
                    if c >= 1:
                        for head in (2 * c - 2, 2 * c - 1):
                            await_stack(act, seg.new, 0, head)
                    elif seg.kind == "loop":
                        for head in (6, 7):
                            await_stack(act, seg.old, 1, head)
                act.activation(dst[:, g * HALF:(g + 1) * HALF], bank[:, :], ACT.Identity, bias=bias[:, c:c + 1])\
                    .then_inc(parts_hi.sem, 1)

            def embed(seg):
                AT = EMBED_SLOTS
                for g in range(2):
                    yield AT[f"xT{g}"]
                    move_T(seg, f"xT{g}", xT[0:FT, g * HALF:(g + 1) * HALF], FT)
                for g in range(2):
                    yield AT[f"zT0.{g}"]
                    move_T(seg, f"zT0.{g}", xnT[:, g * HALF:(g + 1) * HALF])
                for t in range(T):
                    yield AT[f"v0.{t}"]
                    bank, _ = await_filled(act, seg, f"v0.{t}")
                    act.activation(v0[:, t, :, 0:D0], bank[:, :].rearrange("p (h d) -> p h d", d=D0), ACT.Copy)\
                        .then_inc(parts_hi.sem, 1)
                for w, g in HALVES:
                    yield AT[QK0[w, 0, g]]
                    project(seg, 0, w, g)

            def more_heads(seg):
                for c in range(1, NCH):
                    for w, g in HALVES:
                        yield PROJECT_SLOTS[QK0[w, c, g]]
                        project(seg, c, w, g)

            def done_heads(seg):
                for c in range(NCH - 1):
                    for g in range(2):
                        yield TURN_SLOTS[f"oT0.{c}.{g}"]
                        move_T(seg, f"oT0.{c}.{g}", heads_T(c)[:, g * HALF:(g + 1) * HALF])

            def switch(seg):
                b, AT = seg.old, SWITCH_SLOTS
                for g in range(2):
                    yield AT[f"oT1.{g}"]
                    move_T(seg, f"oT1.{g}", xT[:, g * HALF:(g + 1) * HALF])
                for g in range(2):
                    yield AT[f"zT3.{g}"]
                    move_T(seg, f"zT3.{g}", mT[:, g * HALF:(g + 1) * HALF])
                yield AT["route"]
                act.wait_ge(logit_ready.sem, logit_ready.at(b, 1))
                act.activation(ex[:, :, :], ex[:, :, :], ACT.Exp).then_inc(ex_ready.sem, 1)
                for g in range(2):
                    yield AT[f"wT{g}"]
                    move_T(seg, f"wT{g}", xT[0:E, g * HALF:(g + 1) * HALF], E)

            def max_rows(seg, b, layer, head, g):
                bank, drained = await_filled(act, seg, f"m{layer}.{head}.{g}")
                n, k = 8 * layer + head, 2 * (head % 2) + g
                if n >= 2:
                    act.wait_ge(mrow_in[k].sem, mrow_in[k].at(b, 16 * (n // 2)))
                elif seg.kind == "loop":
                    act.wait_ge(mrow_in[k].sem, mrow_in[k].at(seg.old, 16 * 8))
                act.activation(mrow[:, k, :], bank[0:T // 2, 0:P], ACT.Copy, scale=-1.0).then_inc(drained, 1)

            def exps(seg, b, layer, head, g, kt):
                k = 128 * layer + 16 * head + 8 * g + kt
                u = 2 * head + g
                act.wait_ge(score_filled.sem, score_filled.at(b, k + 1))
                if kt == 0:
                    if 32 * layer + 2 * u >= 4:
                        act.wait_ge(o_filled.sem, o_filled.at(b, 32 * layer + 2 * u - 2))
                    elif seg.kind == "loop":
                        act.wait_ge(o_filled.sem, o_filled.at(seg.old, 64 + 2 * u - 2))
                act.activation(pr[:, u % 2, kt, :], score[k % 2][:, :], ACT.Exp, scale=SCALES[layer]).then_inc(exp_done.sem, 1)

            def outputs(b, layer, u, jj):
                D = D0 if layer == 0 else D1
                n = 32 * layer + 2 * u + jj
                act.wait_ge(o_filled.sem, o_filled.at(b, n + 1))
                act.wait_ge(o_drained.sem, o_drained.at(b, n - 1))
                src = obank[n % 2][:, :].rearrange("p (j n) -> p j n", j=2)[:, :, 0:D]
                act.activation(o_hi[:, n % 2, :, 0:D], src, ACT.Copy).then_inc(o_hi_out.sem, 1)

            def attention(seg, b, layer, before_unit, next_head, *beside):
                for head, g, kt, unit, _, rows in steps_of(b, layer, before_unit, next_head):
                    slot = 16 * head + 8 * g + kt
                    exps(seg, b, layer, head, g, kt)
                    if unit and kt in OUT_STEPS:
                        outputs(*unit, OUT_STEPS.index(kt))
                    for row in rows:
                        max_rows(seg, *row)
                    for work in beside:
                        work.run(slot)

            def mlp(seg):
                b = seg.new
                for jj in range(2):
                    outputs(b, 0, 15, jj)
                for g in range(2):
                    move_T(seg, f"oT0.3.{g}", heads_T(3)[:, g * HALF:(g + 1) * HALF])
                for g in range(2):
                    move_T(seg, f"zT1.{g}", zT[:, g * HALF:(g + 1) * HALF])
                for g in range(2):
                    bank, drained = await_filled(act, seg, f"ffn_h{g}")
                    act.activation(xT[:, g * HALF:(g + 1) * HALF], bank[:, :], ACT.Gelu, bias=b1_c).then_inc(drained, 1)
                for g in range(2):
                    move_T(seg, f"zT2.{g}", zT[:, g * HALF:(g + 1) * HALF])
                for w, g in HALVES:
                    dst, bias = (q_hi, bq1_c) if w == "q" else (k_hi, bk1_c)
                    bank, _ = await_filled(act, seg, QK1[w, g])
                    act.activation(dst[:, g * HALF:(g + 1) * HALF], bank[:, :], ACT.Identity, bias=bias)\
                        .then_inc(parts_hi.sem, 1)
                for g in range(2):
                    bank, _ = await_filled(act, seg, f"v1.{g}")
                    act.activation(v1[:, 4 * g:4 * g + 4, :, 0:D1], bank[:, :].rearrange("p (t h d) -> p t h d", t=4, d=D1),
                                   ACT.Copy).then_inc(parts_hi.sem, 1)
                max_rows(seg, b, 1, 0, 0)

            def segment(seg):
                if seg.kind == "first":
                    Beside(embed(seg)).run(LAST_SLOT)
                    max_rows(seg, seg.new, 0, 0, 0)
                    attention(seg, seg.new, 0, None, None, Beside(more_heads(seg)), Beside(done_heads(seg)))
                    mlp(seg)
                elif seg.kind == "loop":
                    attention(seg, seg.old, 1, None, (seg.new, 0, 0), Beside(embed(seg)))
                    attention(seg, seg.new, 0, (seg.old, 1, 15), None,
                              Beside(more_heads(seg)), Beside(done_heads(seg)), Beside(switch(seg)))
                    mlp(seg)
                else:
                    attention(seg, seg.old, 1, None, None)
                    for jj in range(2):
                        outputs(seg.old, 1, 15, jj)
                    Beside(switch(seg)).run(LAST_SLOT)

            segment(Segment("first", 0, NB))
            with act.Fori(0, NB - 1) as i:
                segment(Segment("loop", i, NB))
            segment(Segment("last", 0, NB))

        @block.gpsimd
        def _(pool):
            for n, value in enumerate((-0.5, 1e-5, 1e-6)):
                pool.memset(pool_c[:, n, :], value).then_inc(prep_pool, 1)
            pool.wait_ge(prep_pool, 3)

            def link(seg, ins):
                seg.made += 1
                ins.then_inc(pool_link, 1)
                pool.wait_ge(pool_link, seg.after(POOL_LINKS["first"], POOL_LINKS["loop"], seg.made))

            def rstd(seg, b, n):
                if n == 4:
                    await_drained(pool, seg, "gn_var")
                    var, dst, eps, width = gsm[:, 4:5], gsm[:, 5:6], pool_c[:, 2, 0:1], 1
                else:
                    pool.wait_ge(stats_ready[n].sem, stats_ready[n].at(b, 1))
                    var, dst, eps, width = mv[:, :, 1], rs[:, :], pool_c[:, 1, :], T
                link(seg, pool.tensor_tensor(dst, var, eps, ALU.add))
                pool.tensor_tensor(dst, dst, pool_c[:, 0, 0:width], ALU.pow).then_inc(rstd_ready[n].sem, 1)

            def residual(seg, b, n):
                pool.wait_ge(z_ready[n].sem, z_ready[n].at(b, 2))
                tokens, bias = (h0, h, h)[n], (bo_b, b2_b, bo1_b)[n]
                if n == 0:
                    link(seg, pool.tensor_tensor(tokens[:, :, :], tokens[:, :, :], z[:, :, :], ALU.add))
                pool.tensor_tensor(tokens[:, :, :], tokens[:, :, :], bias[:, :].unsqueeze(1).broadcast_to([P, T, C]), ALU.add)\
                    .then_inc(res_ready.sem, 1)

            def normalize(b, layer, u, jj):
                D, dst = (D0, on) if layer == 0 else (D1, on1)
                head, g = u // 2, u % 2
                n = 32 * layer + 2 * u + jj
                t = 4 * g + 2 * jj
                pool.wait_ge(o_drained.sem, o_drained.at(b, n + 1))
                o = dst[:, t:t + 2, head * D:(head + 1) * D]
                pool.tensor_tensor(o, o, o_r[:, n % 4, :].unsqueeze(2).broadcast_to([P, 2, D]), ALU.mult)\
                    .then_inc(on_ready.sem, 1)

            def embed(seg):
                yield EMBED_SLOTS["ln"]
                rstd(seg, seg.new, 0)
                yield EMBED_SLOTS["z"]
                residual(seg, seg.new, 0)
                yield EMBED_SLOTS["gn_var"]
                rstd(seg, seg.new, 4)

            def switch(seg):
                b, AT = seg.old, SWITCH_SLOTS
                yield AT["ln"]
                rstd(seg, b, 3)
                yield AT["rank"]
                await_drained(pool, seg, "rank")
                for t in range(1, T):
                    pool.tensor_tensor(prefix[:, t, :], prefix[:, t - 1, :], oh[:, t - 1, :], ALU.add)\
                        .then_inc(prefix_ready.sem, 1)
                    pool.wait_ge(prefix_ready.sem, prefix_ready.at(b, t))

            def store(seg):
                b = seg.old
                pool.wait_ge(expert_drained.sem, expert_drained.at(b, 8))
                pool.dma_start(out_v[b.index()], hm[:, :, :]).then_inc(out_stored.sem, 16)
                pool.wait_ge(out_stored.sem, out_stored.at(b, 16))
                pool.sem_inc(hm_free.sem, 1)

            def attention(seg, b, layer, before_unit, next_head, *beside):
                for head, g, kt, unit, _, _ in steps_of(b, layer, before_unit, next_head):
                    if kt in LO_STEPS and (kt - 1) // 2 in POOL_PAIRS:
                        lo_parts(pool, b, layer, 2 * head + g, kt - 1).then_inc(lo_pool.sem, 1)
                    if unit and kt in OUT_STEPS:
                        normalize(*unit, OUT_STEPS.index(kt))
                    for work in beside:
                        work.run(16 * head + 8 * g + kt)

            def mlp(seg):
                for jj in range(2):
                    normalize(seg.new, 0, 15, jj)
                rstd(seg, seg.new, 1)
                residual(seg, seg.new, 1)
                rstd(seg, seg.new, 2)
                residual(seg, seg.new, 2)

            def segment(seg):
                if seg.kind == "first":
                    Beside(embed(seg)).run(LAST_SLOT)
                    attention(seg, seg.new, 0, None, None)
                    mlp(seg)
                elif seg.kind == "loop":
                    attention(seg, seg.old, 1, None, (seg.new, 0, 0), Beside(embed(seg)))
                    attention(seg, seg.new, 0, (seg.old, 1, 15), None, Beside(switch(seg)))
                    mlp(seg)
                    store(seg)
                else:
                    attention(seg, seg.old, 1, None, None)
                    for jj in range(2):
                        normalize(seg.old, 1, 15, jj)
                    Beside(switch(seg)).run(LAST_SLOT)
                    store(seg)
                assert seg.made == POOL_LINKS[seg.kind], (seg.kind, seg.made)

            segment(Segment("first", 0, NB))
            with pool.Fori(0, NB - 1) as i:
                segment(Segment("loop", i, NB))
            segment(Segment("last", 0, NB))

        @block.vector
        def _(dve):
            dve.memset(ones[:, :], 1.0).then_inc(prep_dve, 1)
            dve.memset(kB[64:65, :, :].bitcast(F32), 1.0)
            dve.memset(v0[:, :, :, 2 * D0:2 * D0 + 2], 1.0)
            dve.memset(v1[:, :, :, 2 * D1:2 * D1 + 2], 1.0)
            dve.memset(seen[:, :], 0.0)
            dve.wait_ge(load_small, 16 * N_SMALL)
            for n in range(2):
                last = dve.tensor_tensor(pr[:, 1, 0, n * P:(n + 1) * P], pr[:, 0, 0, n * P:(n + 1) * P], lower, ALU.mult)
            last.then_inc(prep_dve, 1)
            dve.wait_ge(prep_dve, 2)
            for c in range(NCH):
                last = dve.tensor_scalar(pr[:, 1, 1, c * P:(c + 1) * P], ones[:, :], bv_c[:, c:c + 1], None, ALU.mult)
            last.then_inc(prep_dve, 1)
            dve.tensor_scalar(pr[:, 1, 2, 0:P], ones[:, :], bv1_c, None, ALU.mult).then_inc(prep_dve, 1)
            dve.wait_ge(prep_pe, 1)
            for n in range(4):
                dve.tensor_copy(ewT[:, 4 * n:4 * n + 4, :], banks[n][:, :].rearrange("p (e f) -> p e f", f=P))
            dve.tensor_copy(w1T[:, :], banks[4][:, 0:P])
            dve.tensor_copy(w2T[:, :], banks[4][:, P:2 * P])
            dve.tensor_copy(swT[:, :], banks[4][:, 2 * P:2 * P + E])
            dve.tensor_copy(bo_b[:, :], banks[5][:, 0:P])
            dve.tensor_copy(bo1_b[:, :], banks[6][:, 0:P])
            dve.tensor_copy(b2_b[:, :], banks[7][:, 0:P])
            dve.tensor_copy(sb_b[:, :], banks[7][:, P:P + E]).then_inc(prep_dve, 1)
            dve.wait_ge(prep_dve, PREP_DVE)
            dve.sem_inc(glue_drained[0], 1)
            dve.sem_inc(glue_drained[1], 1)
            dve.sem_inc(max_reduced.sem, 2)
            dve.sem_inc(exp_done.sem, 2)
            dve.sem_inc(o_drained.sem, 2)
            dve.sem_inc(hm_free.sem, 1)

            def mark(seg, ins):
                seg.made += 1
                ins.then_inc(dve_link, 1)

            def settle(seg, behind=0):
                dve.wait_ge(dve_link, seg.after(DVE_LINKS["first"], DVE_LINKS["loop"], seg.made - behind))

            def link(seg, ins):
                mark(seg, ins)
                settle(seg)

            def bank_tiles(bank):
                return bank[:, :].rearrange("p (t c) -> p t c", t=4)

            def norm_stats(seg, n, tokens):
                for t in range(T):
                    ins = dve.bn_stats(st[:, t, :], tokens[:, t, :])
                link(seg, ins)
                dve.memset(gsm[:, 7:8], 0.0)
                for t in range(T):
                    ins = dve.bn_aggr(mv[:, t, :], st[:, t, :])
                ins.then_inc(stats_ready[n].sem, 1)

            def norm_apply(b, n, tokens, halves=(0, 1)):
                if halves[0] == 0:
                    dve.wait_ge(stats_ready[n].sem, stats_ready[n].at(b, 1))
                    dve.wait_ge(rstd_ready[n].sem, rstd_ready[n].at(b, 1))
                for g in halves:
                    for j in range(4):
                        t = 4 * g + j
                        ins = dve.tensor_scalar(z[:, t, :], tokens[:, t, :], mv[:, t, 0:1], rs[:, t:t + 1],
                                                ALU.subtract, ALU.mult)
                    ins.then_inc(z_ready[n].sem, 1)

            def add_result(seg, name, g, dst, base):
                bank, drained = await_filled(dve, seg, name)
                half = slice(4 * g, 4 * g + 4)
                dve.tensor_tensor(dst[:, half, :], bank_tiles(bank), base[:, half, :], ALU.add).then_inc(drained, 1)

            def lo_part(seg, name, b, hi_count, hi, lo, g, bias):
                bank, drained = await_filled(dve, seg, name)
                dve.wait_ge(parts_hi.sem, parts_hi.at(b, hi_count))
                sl = slice(g * HALF, (g + 1) * HALF)
                dve.scalar_tensor_tensor(lo[:, sl], bank[:, :], bias, hi[:, sl].bitcast(F32), ALU.add, ALU.subtract)\
                    .then_inc(drained, 1)

            def project(seg, c, w, g):
                hi, lo, bias = (q_hi, q_lo, bq_c) if w == "q" else (k_hi, k_lo, bk_c)
                lo_part(seg, QK0[w, c, g], seg.new, 8 + 4 * c + 2 * (w == "k") + g + 1, hi, lo, g, bias[:, c:c + 1])

            def embed(seg):
                b, AT = seg.new, EMBED_SLOTS
                for g in range(2):
                    yield AT[f"h{g}"]
                    add_result(seg, f"h{g}", g, h0, pe_sb)
                yield AT["ln"]
                await_drained(dve, seg, "h0", "h1")
                norm_stats(seg, 0, h0)
                yield AT["z"]
                norm_apply(b, 0, h0)
                yield AT["gn"]
                await_drained(dve, seg, "zT0.0", "zT0.1")
                for g in range(2):
                    ins = dve.bn_stats(gst[:, g, :], xnT[:, g * HALF:(g + 1) * HALF])
                link(seg, ins)
                dve.memset(gsm[:, 7:8], 0.0)
                link(seg, dve.bn_aggr(gmv[:, :], gst[:, :, :].rearrange("p a b -> p (a b)")))
                dve.tensor_copy(gsm[:, 0:1], gmv[:, 0:1]).then_inc(gn_stat.sem, 1)
                yield AT["gn_mean"] + 1
                bank, drained = await_filled(dve, seg, "gn_mean")
                dve.tensor_copy(gsm[:, 2:3], bank[:, 0:1]).then_inc(drained, 1)
                await_drained(dve, seg, "gn_mean")
                link(seg, dve.tensor_tensor(gsm[:, 3:4], gmv[:, 0:1], gsm[:, 2:3], ALU.subtract))
                dve.scalar_tensor_tensor(gsm[:, 1:2], gsm[:, 3:4], gsm[:, 3:4], gmv[:, 1:2], ALU.mult, ALU.add)\
                    .then_inc(gn_stat.sem, 1)
                yield AT["gn_var"]
                bank, drained = await_filled(dve, seg, "gn_var")
                dve.tensor_copy(gsm[:, 4:5], bank[:, 0:1]).then_inc(drained, 1)
                yield AT["xn"]
                dve.wait_ge(rstd_ready[4].sem, rstd_ready[4].at(b, 1))
                link(seg, dve.tensor_tensor(gsm[:, 6:7], gsm[:, 5:6], gnw_c, ALU.mult))
                link(seg, dve.tensor_tensor(gsm[:, 3:4], gsm[:, 2:3], gsm[:, 6:7], ALU.mult))
                link(seg, dve.tensor_tensor(gsm[:, 7:8], gnb_c, gsm[:, 3:4], ALU.subtract))
                dve.tensor_scalar(xnT[:, :], xnT[:, :], gsm[:, 6:7], gsm[:, 7:8], ALU.mult, ALU.add).then_inc(xn_ready.sem, 1)
                for t in range(T):
                    yield AT[f"v0.{t}"] + 1
                    bank, drained = await_filled(dve, seg, f"v0.{t}")
                    dve.wait_ge(parts_hi.sem, parts_hi.at(b, t + 1))
                    dve.tensor_tensor(v0[:, t, :, D0:2 * D0], bank[:, :].rearrange("p (h d) -> p h d", d=D0),
                                      v0[:, t, :, 0:D0], ALU.subtract).then_inc(drained, 1)
                for w, g in HALVES:
                    yield AT[QK0[w, 0, g]] + 1
                    project(seg, 0, w, g)

            def more_heads(seg):
                for c in range(1, NCH):
                    for w, g in HALVES:
                        yield PROJECT_SLOTS[QK0[w, c, g]] + 1
                        project(seg, c, w, g)

            def switch(seg):
                b, AT = seg.old, SWITCH_SLOTS
                for g in range(2):
                    yield AT[f"attn1.{g}"]
                    if g == 0:
                        dve.wait_ge(res_ready.sem, res_ready.at(b, 3))
                        dve.wait_ge(hm_free.sem, hm_free.at(b, 0))
                    add_result(seg, f"attn1.{g}", g, hm, h)
                yield AT["ln"]
                await_drained(dve, seg, "attn1.0", "attn1.1")
                norm_stats(seg, 3, hm)
                yield AT["z"]
                if seg.kind == "loop":
                    dve.wait_ge(res_ready.sem, res_ready.at(seg.new, 1))
                norm_apply(b, 3, hm)
                def over_e(a):
                    return a.unsqueeze(2).broadcast_to([P, T, E])
                top, total, rp, vm, pos, kr, un = (small[:, n, :] for n in range(7))
                yield AT["logits"]
                bank, drained = await_filled(dve, seg, "logits")
                dve.tensor_tensor(lg[:, :, :], bank[:, 0:T * E].rearrange("p (t e) -> p t e", e=E),
                                  sb_b[:, :].unsqueeze(1).broadcast_to([P, T, E]), ALU.add).then_inc(drained, 1)
                await_drained(dve, seg, "logits")
                link(seg, dve.tensor_reduce(top, lg[:, :, :], AX_X, ALU.max))
                dve.tensor_tensor(ex[:, :, :], lg[:, :, :], over_e(top), ALU.subtract).then_inc(logit_ready.sem, 1)
                link(seg, dve.tensor_tensor(oh[:, :, :], lg[:, :, :], over_e(top), ALU.is_equal))
                yield AT["route"]
                link(seg, dve.tensor_tensor(lg[:, :, :], oh[:, :, :], desc.rearrange("p (t e) -> p t e", e=E), ALU.mult))
                link(seg, dve.tensor_reduce(vm, lg[:, :, :], AX_X, ALU.max))
                link(seg, dve.tensor_tensor(oh[:, :, :], lg[:, :, :], over_e(vm), ALU.is_equal))
                dve.tensor_reduce(per_p[:, :], oh[:, :, :].rearrange("p t e -> p e t"), AX_X, ALU.add).then_inc(oh_ready.sem, 1)
                yield AT["rank"]
                dve.wait_ge(ex_ready.sem, ex_ready.at(b, 1))
                link(seg, dve.tensor_reduce(total, ex[:, :, :], AX_X, ALU.add))
                link(seg, dve.reciprocal(rp, total))
                bank, drained = await_filled(dve, seg, "rank")
                link(seg, dve.tensor_tensor(prefix[:, 0, :], bank[:, 0:E], seen[:, :], ALU.add))
                dve.tensor_tensor(seen[:, :], bank[:, E:2 * E], seen[:, :], ALU.add).then_inc(drained, 1)
                yield AT["place"]
                dve.wait_ge(prefix_ready.sem, prefix_ready.at(b, 7))
                link(seg, dve.tensor_tensor(lg[:, :, :], oh[:, :, :], prefix[:, :, :], ALU.mult))
                link(seg, dve.tensor_reduce(pos, lg[:, :, :], AX_X, ALU.add))
                link(seg, dve.scalar_tensor_tensor(kr, pos, CAP, rp, ALU.is_lt, ALU.mult))
                link(seg, dve.tensor_tensor(un, rp, kr, ALU.subtract))
                dve.tensor_tensor(wgt[:, :, :], oh[:, :, :], over_e(kr), ALU.mult).then_inc(wgt_ready.sem, 1)
                for t in range(T):
                    ins = dve.scalar_tensor_tensor(hm[:, t, :], z[:, t, :], un[:, t:t + 1], hm[:, t, :], ALU.mult, ALU.add)
                link(seg, ins)
                for g in range(2):
                    yield AT[f"eb{g}"]
                    add_result(seg, f"eb{g}", g, hm, hm)
                def experts(dst, t0, q, done):
                    for e in range(4):
                        for d in range(2):
                            t = t0 + d
                            if e > 0:
                                settle(seg, 0 if (e, d) == (3, 1) and done[0] else 1)
                            ins = dve.scalar_tensor_tensor(hm[:, t, :], dst[d][:, e * P:(e + 1) * P],
                                                           wgt[:, t, 4 * q + e:4 * q + e + 1], hm[:, t, :], ALU.mult, ALU.add)
                            if e == 3 and done[d]:
                                ins.then_inc(done[d], 1)
                            else:
                                mark(seg, ins)

                for n in range(8):
                    yield AT[f"e{n}.0"]
                    if n == 0:
                        await_drained(dve, seg, "eb0", "eb1")
                    elif n % 4 > 0:
                        await_drained(dve, seg, f"e{n - 1}.0", f"e{n - 1}.1")
                    both = [await_filled(dve, seg, f"e{n}.{d}") for d in range(2)]
                    experts([bank for bank, _ in both], 2 * (n // 4), n % 4, [drained for _, drained in both])
                for n, slot in enumerate(EXPERT_SLOTS):
                    yield slot
                    if n % 4 > 0:
                        dve.wait_ge(expert_drained.sem, expert_drained.at(b, n))
                    dve.wait_ge(expert_filled.sem, expert_filled.at(b, n + 1))
                    experts(maxb, 4 + 2 * (n // 4), n % 4, [None, expert_drained.sem])

            def max_tile(b, layer, head, n):
                k = 128 * layer + 16 * head + n
                dve.wait_ge(max_filled.sem, max_filled.at(b, k + 1))
                dve.tensor_reduce(mxh[:, head % 2, n // 2, n % 2:n % 2 + 1], maxb[k % 2][:, :], AX_X, ALU.max)\
                    .then_inc(max_reduced.sem, 1)
                if n % 8 == 7:
                    half = slice(n // 8 * T // 2, (n // 8 + 1) * T // 2)
                    dve.wait_ge(max_reduced.sem, max_reduced.at(b, k + 1))
                    dve.tensor_reduce(mx[:, head % 2, half], mxh[:, head % 2, half, :], AX_X, ALU.max).then_inc(max_ready.sem, 1)

            def lo_pair(b, layer, u, kt):
                if kt // 2 not in POOL_PAIRS:
                    lo_parts(dve, b, layer, u, kt).then_inc(lo_done.sem, 1)

            def outputs(b, layer, u, jj):
                D, dst = (D0, on) if layer == 0 else (D1, on1)
                n = 32 * layer + 2 * u + jj
                head, t = u // 2, 4 * (u % 2) + 2 * jj
                dve.wait_ge(o_hi_out.sem, o_hi_out.at(b, n + 1))
                bank = obank[n % 2][:, :].rearrange("p (j n) -> p j n", j=2)
                if n >= 4:
                    dve.wait_ge(on_ready.sem, on_ready.at(b, n - 3))
                dve.reciprocal(o_r[:, n % 4, :], bank[:, :, 2 * D])
                dve.tensor_tensor(dst[:, t:t + 2, head * D:(head + 1) * D], bank[:, :, D:2 * D],
                                  o_hi[:, n % 2, :, 0:D], ALU.add).then_inc(o_drained.sem, 1)

            def attention(seg, b, layer, before_unit, next_head, *beside):
                for head, g, kt, unit, tiles, _ in steps_of(b, layer, before_unit, next_head):
                    slot = 16 * head + 8 * g + kt
                    if kt in LO_STEPS:
                        lo_pair(b, layer, 2 * head + g, kt - 1)
                    elif kt == 0 and unit:
                        lo_pair(*unit, T - 1)
                    for tile in tiles:
                        max_tile(*tile)
                    if unit and kt in OUT_STEPS:
                        outputs(*unit, OUT_STEPS.index(kt))
                    for work in beside:
                        work.run(slot)

            def mlp(seg, *beside):
                b = seg.new

                def catch_up(name):
                    for work in beside:
                        work.run(MLP_SLOTS[name])

                lo_pair(b, 0, 15, T - 1)
                catch_up("start")
                for jj in range(2):
                    outputs(b, 0, 15, jj)
                dve.wait_ge(res_ready.sem, res_ready.at(b, 1))
                for g in range(2):
                    catch_up(f"attn0.{g}")
                    add_result(seg, f"attn0.{g}", g, h, h0)
                await_drained(dve, seg, "attn0.0", "attn0.1")
                norm_stats(seg, 1, h)
                catch_up("ln1")
                norm_apply(b, 1, h)
                dve.memset(kA[64:65, :, :].bitcast(F32), 1.0)
                dve.wait_ge(res_ready.sem, res_ready.at(b, 2))
                for g in range(2):
                    catch_up(f"ffn_o{g}")
                    add_result(seg, f"ffn_o{g}", g, h, h)
                await_drained(dve, seg, "ffn_o0", "ffn_o1")
                norm_stats(seg, 2, h)
                catch_up("ln2")
                norm_apply(b, 2, h)
                for w, g in HALVES:
                    catch_up(QK1[w, g])
                    hi, lo, bias = (q_hi, q_lo, bq1_c) if w == "q" else (k_hi, k_lo, bk1_c)
                    lo_part(seg, QK1[w, g], b, 8 + 16 + 2 * (w == "k") + g + 1, hi, lo, g, bias)
                for g in range(2):
                    catch_up(f"v1.{g}")
                    bank, drained = await_filled(dve, seg, f"v1.{g}")
                    dve.wait_ge(parts_hi.sem, parts_hi.at(b, 29 + g))
                    v = v1[:, 4 * g:4 * g + 4, :, :]
                    src = bank[:, :].rearrange("p (t h d) -> p t h d", t=4, d=D1)
                    dve.tensor_tensor(v[:, :, :, D1:2 * D1], src, v[:, :, :, 0:D1], ALU.subtract).then_inc(drained, 1)
                catch_up("max")
                for n in EARLY_TILES[1]:
                    max_tile(b, 1, 0, n)

            def segment(seg):
                if seg.kind == "first":
                    Beside(embed(seg)).run(LAST_SLOT)
                    for n in EARLY_TILES[0]:
                        max_tile(seg.new, 0, 0, n)
                    attention(seg, seg.new, 0, None, None, Beside(more_heads(seg)))
                    mlp(seg)
                elif seg.kind == "loop":
                    attention(seg, seg.old, 1, None, (seg.new, 0, 0), Beside(embed(seg)))
                    switched = Beside(switch(seg))
                    attention(seg, seg.new, 0, (seg.old, 1, 15), None, Beside(more_heads(seg)), switched)
                    mlp(seg, switched)
                else:
                    attention(seg, seg.old, 1, None, None)
                    lo_pair(seg.old, 1, 15, T - 1)
                    for jj in range(2):
                        outputs(seg.old, 1, 15, jj)
                    Beside(switch(seg)).run(LAST_SLOT)
                assert seg.made == DVE_LINKS[seg.kind], (seg.kind, seg.made)

            segment(Segment("first", 0, NB))
            with dve.Fori(0, NB - 1) as i:
                segment(Segment("loop", i, NB))
            segment(Segment("last", 0, NB))


LAST_SLOT = max(MLP_SLOTS.values())
POOL_PAIRS = (0,)
LO_STEPS = (2, 4, 6)
VALUE_STEPS = (2, 3, 5, 6)
OUT_STEPS = (4, 7)
SCALES = (64 ** -0.5, 1.0 / math.sqrt(16))
N_SMALL = 29
PREP_DVE = 5
DVE_LINKS = {"first": 9, "loop": 127, "last": 118}
POOL_LINKS = {"first": 5, "loop": 6, "last": 1}

_INS = ['x', 'L0_tok_W', 'L0_attn_gn_w', 'L0_attn_gn_b', 'L0_attn_wq', 'L0_attn_bq', 'L0_attn_wk', 'L0_attn_bk',
        'L0_attn_wv', 'L0_attn_bv', 'L0_attn_wo', 'L0_attn_bo', 'L0_ffn_W1', 'L0_ffn_b1', 'L0_ffn_W2', 'L0_ffn_b2',
        'L1_attn_Wq', 'L1_attn_Wk', 'L1_attn_Wv', 'L1_attn_bq', 'L1_attn_bk', 'L1_attn_bv', 'L1_attn_Wo', 'L1_attn_bo',
        'L1_ffn_switch_w', 'L1_ffn_switch_b', 'L1_ffn_expert_w', 'L1_ffn_expert_b']


def shape_tables(S, C, E):
    position = np.arange(2 * S, dtype=np.float32)[:, None]
    div_term = np.exp(np.arange(0, C, 2, dtype=np.float32) * (-math.log(10000.0) / C))
    pe = np.zeros((2 * S, C), dtype=np.float32)
    pe[:, 0::2] = np.sin(position * div_term)
    pe[:, 1::2] = np.cos(position * div_term)
    r = np.arange(P)
    tri = np.stack([
        np.eye(P), (r[:, None] // 4 == r[None, :] // 4) / 4.0, r[:, None] < r[None, :], r[:, None] >= r[None, :],
        np.broadcast_to(E - (r % E), (P, P)),
    ], axis=1).astype(np.float32)
    return pe[:S].reshape(P, S // P, C), tri


def kernel(**inputs):
    import concourse.bacc as _bacc
    from concourse.bass_utils import run_bass_kernel_spmd as _run

    nc = _bacc.Bacc("TRN2", target_bir_lowering=False, num_devices=1)
    arrays, args = {}, []
    for name in _INS:
        a = np.ascontiguousarray(inputs[name])
        arrays[f"in_{name}"] = a
        args.append(nc.dram_tensor(f"in_{name}", a.shape, mybir.dt.from_np(a.dtype), kind="ExternalInput").ap())
    for name, a in zip(("pe", "tri"), shape_tables(1024, 128, 16)):
        a = np.ascontiguousarray(a)
        arrays[f"in_{name}"] = a
        args.append(nc.dram_tensor(f"in_{name}", a.shape, mybir.dt.from_np(a.dtype), kind="ExternalInput").ap())
    nb = inputs["x"].shape[0]
    out = nc.dram_tensor("out_0", (nb, 1024, 128), F32, kind="ExternalOutput").ap()
    build(nc, *args, out)
    r = _run(nc, [arrays], core_ids=[0])
    return r.results[0]["out_0"]
```
